# Optimizing a Trainium2 kernel written in Bass

```python
import numpy as np
import jax
import jax.numpy as jnp

def _softmax(x, axis=-1):
    return jax.nn.softmax(x, axis=axis)

def _gelu(x):
    return jax.nn.gelu(x, approximate=True)

def _silu(x):
    return jax.nn.silu(x)

def _sigmoid(x):
    return jax.nn.sigmoid(x)

def _layernorm(x, axis=-1, eps=1e-05):
    m = jnp.mean(x, axis=axis, keepdims=True)
    v = jnp.var(x, axis=axis, keepdims=True)
    return (x - m) / jnp.sqrt(v + eps)

def _scatter_add(tgt, idx, src, axis=0):
    return tgt.at[idx].add(src)

def _segment_sum(src, seg, n):
    return jax.ops.segment_sum(src, seg, n)
kernel_name = 'mk_adj_resnorm_d1_adj_r2_5f8afa'

def setup_inputs(seed: int=0):
    np.random.seed(seed)
    _w = jnp.asarray

    def _rec_inputs():
        import jax
        import jax.numpy as jnp
        _gk = jax.random.key(seed)
        x = -0.0005207 + 1.001 * jax.random.normal(jax.random.fold_in(_gk, 1), (4096, 256), jnp.float32)
        _w = (1.0 + jnp.arange(4096, dtype=jnp.float32)) ** (-0.5)
        _w = _w / _w.mean()
        _pij = jnp.clip(0.00390625 * _w[:, None] * _w[None, :], 0.0, 1.0)
        _a = jax.random.uniform(jax.random.fold_in(_gk, 2), (4096, 4096)) < _pij
        adj = _a.astype(jnp.int32)
        return (x, adj)
    x, adj = _rec_inputs()

    def _L0_gnn_setup():
        import jax, jax.numpy as jnp
        import numpy as np
        N = 2048
        IN_FEAT = 256
        EMBED = 256
        HEADS = 8
        HEAD_DIM = EMBED // HEADS
        SCALING = HEAD_DIM ** (-0.5)
        key = jax.random.key(seed)
        ks = jax.random.split(key, 7)
        x = jax.random.normal(ks[0], (N, IN_FEAT), dtype=jnp.float32)
        adj = jax.random.randint(ks[1], (N, N), 0, 2, dtype=jnp.int32)
        s = 0.04
        WQ = jax.random.normal(ks[2], (EMBED, IN_FEAT), dtype=jnp.float32) * s
        WK = jax.random.normal(ks[3], (EMBED, IN_FEAT), dtype=jnp.float32) * s
        WV = jax.random.normal(ks[4], (EMBED, IN_FEAT), dtype=jnp.float32) * s
        we = jax.random.normal(ks[5], (1, HEAD_DIM), dtype=jnp.float32) * 0.1
        be = jnp.zeros((1,), dtype=jnp.float32)
        return {'x': x, 'adj': adj, 'WQ': WQ, 'WK': WK, 'WV': WV, 'we': we, 'be': be}
    _L0_gnn_all = _L0_gnn_setup()
    _L0_gnn_in = {k: v for k, v in _L0_gnn_all.items() if k in ('WQ', 'WK', 'WV', 'we', 'be')}
    del _L0_gnn_all
    return {'x': x, 'adj': adj, 'L0_gnn_WQ': _L0_gnn_in['WQ'], 'L0_gnn_WK': _L0_gnn_in['WK'], 'L0_gnn_WV': _L0_gnn_in['WV'], 'L0_gnn_we': _L0_gnn_in['we'], 'L0_gnn_be': _L0_gnn_in['be']}

def reference(x, adj, L0_gnn_WQ, L0_gnn_WK, L0_gnn_WV, L0_gnn_we, L0_gnn_be):
    import jax
    import jax.numpy as jnp

    def _L0_gnn_ref(x, adj, WQ, WK, WV, we, be):
        import jax, jax.numpy as jnp
        import numpy as np
        N = 2048
        IN_FEAT = 256
        EMBED = 256
        HEADS = 8
        HEAD_DIM = EMBED // HEADS
        SCALING = HEAD_DIM ** (-0.5)
        n = x.shape[0]
        Q = (x @ WQ.T).reshape(n, HEADS, HEAD_DIM).transpose(1, 0, 2)
        K = (x @ WK.T).reshape(n, HEADS, HEAD_DIM).transpose(1, 0, 2)
        V = (x @ WV.T).reshape(n, HEADS, HEAD_DIM).transpose(1, 0, 2)
        energy = Q @ we.T + be
        attn = jnp.einsum('hqd,hkd->hqk', Q, K) * SCALING + energy
        attn = attn + jnp.where(adj > 0, 0.0, -jnp.inf)
        attn = jax.nn.softmax(attn, axis=-1)
        hard = (attn == jnp.max(attn, axis=-1, keepdims=True)).astype(jnp.float32) / HEADS
        out = jnp.einsum('hqk,hkd->hqd', hard, V)
        return out.transpose(1, 0, 2).reshape(n, EMBED)
    x = _layernorm(x + _L0_gnn_ref(x, adj, L0_gnn_WQ, L0_gnn_WK, L0_gnn_WV, L0_gnn_we, L0_gnn_be), axis=-1)
    return x

_drawn_inputs = setup_inputs


def setup_inputs(seed=0):
    import zlib

    import numpy as np

    out = dict(_drawn_inputs(seed))
    spreads = {}
    factors = {}
    for name, (base, spread) in spreads.items():
        noise = np.random.default_rng([zlib.crc32(name.encode()), seed]).standard_normal(out[name].shape)
        drawn = base * np.exp(spread * noise) if base else spread * noise
        out[name] = jnp.asarray(drawn.astype(out[name].dtype))
    for name, factor in factors.items():
        out[name] = (out[name] * factor).astype(out[name].dtype)
    return out
```

```python
from contextlib import ExitStack

import concourse.bass as bass
from concourse import mybir

ALU = mybir.AluOpType
ACT = mybir.ActivationFunctionType
AX = mybir.AxisListType
F32 = mybir.dt.float32
BF16 = mybir.dt.bfloat16
F16 = mybir.dt.float16
I32 = mybir.dt.int32
U32 = mybir.dt.uint32

P = 128
HD = 32
PARTS = 3
CHUNKS = 4
SLOTS = CHUNKS * P
RING = 3
TABLES = 4
EPS = 1e-5
BIG = 2.0 ** 100
FLOOR = -(2.0 ** 90)


def hard_attention(nc, x, adj, wq, wk, wv, we, be, out):
    N, D = x.shape
    H = D // HD
    T = N // P
    NB = N // P
    HALVES = D // P
    PAIRS = H // 2
    HP = PARTS * HD
    KW = H * HP
    ROW = 2 * KW
    MAX_ITEMS = T * (N // SLOTS)
    GT = 4
    G = T // GT
    SCALE = float(HD) ** -0.5
    assert D == 256 and N == 4096 and SLOTS == 512 and H == 8

    kv_table = nc.dram_tensor("kv_table", (N + 1, ROW), BF16, kind="Internal").ap()
    mask_table = [nc.dram_tensor(f"mask_table{i}", (N + 1, P), BF16, kind="Internal").ap() for i in range(TABLES)]
    q_table = nc.dram_tensor("q_table", (T, PARTS, HD, H, P), BF16, kind="Internal").ap()

    with ExitStack() as ctx:
        def sb(name, shape, dt):
            return ctx.enter_context(nc.sbuf_tensor(name, shape, dt))

        def pb(name, dt=F32):
            return ctx.enter_context(nc.psum_tensor(name, [P, 512], dt))

        def sem(name):
            return ctx.enter_context(nc.semaphore(name))

        ident_f = sb("ident_f", [P, P], F32)
        ident_b = sb("ident_b", [P, P], BF16)
        ident_big = sb("ident_big", [P, P], BF16)
        before = sb("before", [P, P], F32)
        ones_f = sb("ones_f", [P, P], F32)
        ones_b = sb("ones_b", [P, 1], BF16)
        iota_chunk = sb("iota_chunk", [P, NB], I32)
        iota_slot = sb("iota_slot", [P, P], I32)
        slot_id = sb("slot_id", [P, NB], I32)
        key_c = sb("key_c", [P, NB], I32)
        iota_chunk_h = sb("iota_chunk_h", [P, NB], F16)
        iota_slot_h = sb("iota_slot_h", [P, P], F16)
        key_h = sb("key_h", [P, NB], F16)
        be_sb = sb("be_sb", [P, 1], F32)
        we_sb = sb("we_sb", [P, D], F32)
        zeros = sb("zeros", [P, ROW], BF16)
        minus_half = sb("minus_half", [P, 1], F32)
        eps = sb("eps", [P, 1], F32)
        masked = sb("masked", [1, P], BF16)
        w_sb = [sb(f"w{i}", [P, HALVES, D], F32) for i in range(3)]
        w_t = [sb(f"wt{i}", [P, HALVES, D], F32) for i in range(3)]
        x_in = [sb(f"x_in{i}", [P, GT, D], F32) for i in range(2)]
        x_t = sb("x_t", [P, HALVES, GT * P], F32)
        q_out = [sb(f"q_out{i}", [P, GT, HALVES, P], BF16) for i in range(PARTS)]
        q_rest = [sb(f"q_rest{i}", [P, GT * P], F32) for i in range(HALVES)]
        kv_out = [sb(f"kv_out{i}", [P, ROW], BF16) for i in range(2)]
        kv_f = [sb(f"kv_f{i}", [P, 2 * D], F32) for i in range(2)]
        kv_rest = [sb(f"kv_rest{i}", [P, 2 * D], F32) for i in range(2)]
        adj_in = sb("adj_in", [P, N], I32)
        joined = sb("joined", [P, N], BF16)
        joined_t = sb("joined_t", [P, NB, P], BF16)
        flag = sb("flag", [P, NB], F32)
        ones_nb = sb("ones_nb", [P, NB], F32)
        prefix = sb("prefix", [P, NB], F32)
        rank1 = sb("rank1", [P, NB], F32)
        rank = sb("rank", [P, NB], I32)
        digits = sb("digits", [P, 2, NB], I32)
        digits_h = sb("digits_h", [P, 2, NB], F16)
        hot_hi = sb("hot_hi", [P, NB, NB], F16)
        hot_key = sb("hot_key", [P, NB, NB], F16)
        hot_lo = sb("hot_lo", [P, NB, P], F16)
        total_i = sb("total_i", [P, 1], I32)
        n_items = sb("n_items", [P, T], I32)
        unused = sb("unused", [P, NB], F32)
        list_f = sb("list_f", [P, NB], F32)
        lists = sb("lists", [P, TABLES * NB], U32)
        picks = [sb(f"picks{i}", [P, CHUNKS], U32) for i in range(RING)]
        kv = [sb(f"kv{i}", [P, CHUNKS, ROW], BF16) for i in range(RING)]
        mrow = [sb(f"mrow{i}", [P, CHUNKS, P], BF16) for i in range(RING)]
        k_t = [sb(f"k_t{i}", [HP, H, SLOTS], BF16) for i in range(RING)]
        mask = [sb(f"mask{i}", [P, SLOTS], F32) for i in range(RING)]
        q_next = sb("q_next", [HP, PARTS, H, P], BF16)
        q_cur = sb("q_cur", [HP, PARTS, H, P], BF16)
        score = [sb(f"score{i}", [P, SLOTS], F32) for i in range(4)]
        hard = [sb(f"hard{i}", [P, SLOTS], BF16) for i in range(4)]
        hard_t = [sb(f"hard_t{i}", [P, 2 * SLOTS], BF16) for i in range(2)]
        top = [sb(f"top{i}", [P, H], F32) for i in range(RING)]
        keep = sb("keep", [P, H], F32)
        o_item = sb("o_item", [P, H, HD], F32)
        o_run = sb("o_run", [P, H, HD], F32)
        x_row = sb("x_row", [P, D], F32)
        y = sb("y", [P, D], F32)
        stats = sb("stats", [P, 6], F32)
        mean_var = sb("mean_var", [P, 2], F32)
        std = sb("std", [P, 1], F32)
        rstd = sb("rstd", [P, 1], F32)
        y_out = sb("y_out", [P, D], F32)

        ps_s = [pb("ps_s0"), pb("ps_s1")]
        ps_t = [pb("ps_t0"), pb("ps_t1")]
        ps_o = [pb("ps_o0"), pb("ps_o1")]
        ps_k = pb("ps_k")
        ps_fe = pb("ps_fe")

        def as_bf16(bank):
            return bank[:].bitcast(BF16)

        def heads(cols):
            return cols[:].rearrange("p (h d) -> p h d", d=HD)

        def head_rows(row, part):
            return row[:].rearrange("p (h s d) -> p h s d", s=PARTS, d=HD)[:, :, part, :]

        HIGH, MID, LOW = 0, 1, 2

        ld_w, ld_c, ld_x, ld_x0, ld_q = (
            sem("ld_w"), sem("ld_c"), [sem("ld_x_even"), sem("ld_x_odd")], sem("ld_x0"), sem("ld_q"))
        ld_adj = sem("ld_adj")
        pool_c, dve_c = sem("pool_c"), sem("dve_c")
        pe_w, dve_w = sem("pe_w"), sem("dve_w")
        pe_xt, xt_copied = sem("pe_xt"), sem("xt_copied")
        pe_q, st_q = sem("pe_q"), sem("st_q")
        q_hi, q_rested, q_mid, q_low = sem("q_hi"), sem("q_rested"), sem("q_mid"), sem("q_low")
        pe_k, pe_v, k_done, v_copied, kv_hi, kv_rested, kv_mid, kv_low = (
            sem("pe_k"), sem("pe_v"), sem("k_done"), sem("v_copied"), sem("kv_hi"), sem("kv_rested"),
            sem("kv_mid"), sem("kv_low"))
        st_kv = [sem("st_kv0"), sem("st_kv1")]
        st_c = sem("st_c")
        act_cast, pe_jt, act_jt, pe_cnt, dve_fe, pe_base, pe_list, st_mask, lists_read = (
            sem("act_cast"), sem("pe_jt"), sem("act_jt"), sem("pe_cnt"), sem("dve_fe"), sem("pe_base"),
            sem("pe_list"), sem("st_mask"), sem("lists_read"))
        picked = sem("picked")
        landed = [sem(f"landed{i}") for i in range(RING)]
        pe_kt, act_kt, pe_mask, act_mask = sem("pe_kt"), sem("act_kt"), sem("pe_mask"), sem("act_mask")
        pe_score, dve_top, dve_hard, pe_hard_t, act_hard_t, pe_pv = (
            sem("pe_score"), sem("dve_top"), sem("dve_hard"), sem("pe_hard_t"), sem("act_hard_t"), sem("pe_pv"))
        dve_osum, dve_merge, dve_keep, q_ready = sem("dve_osum"), sem("dve_merge"), sem("dve_keep"), sem("q_ready")
        dve_ln, act_std, st_out = sem("dve_ln"), sem("act_std"), sem("st_out")
        A_TOP, A_HT, A_HC, A_PV = 2, 4, 4, 16
        QLOAD = 16 * PARTS

        block = ctx.enter_context(nc.Block())

        scratch = {}

        def wait_alone(eng, *waits):
            regs = scratch.setdefault(str(eng.engine), [eng.alloc_register(f"wait{i}") for i in range(2)]
                                      if str(eng.engine) not in scratch else None)
            for (_, value), reg in zip(waits, regs):
                eng.reg_mov(reg, value)
            eng.wait_ge(dve_c, 1)
            for (waited, _), reg in zip(waits, regs):
                eng.wait_ge(waited, reg)

        def run_items(eng, item, inner, tiles=T, closing=None):
            r = {k: eng.alloc_register(k) for k in ("n8", "m", "nm", "t", "off")}
            for k in r:
                eng.reg_mov(r[k], 0)
            with eng.Fori(0, MAX_ITEMS // RING + 1) as it:
                with eng.If(eng.snap(r["t"]) < tiles + (closing is not None)):
                    for b in range(RING):
                        with eng.If(eng.snap(r["m"]) < 1):
                            if closing is not None:
                                with eng.If(eng.snap(r["m"]) < -99):
                                    closing(b, eng.snap(r["n8"]))
                                    eng.reg_mov(r["m"], -50)
                                    eng.reg_add(r["t"], r["t"], 1)
                            with eng.If(eng.snap(r["m"]) > -1):
                                inner(r)
                                item(b, True, r, it)
                        with eng.If(eng.snap(r["m"]) > 0):
                            item(b, False, r, it)
                        eng.reg_add(r["n8"], r["n8"], 8)
                        eng.reg_add(r["m"], r["m"], 1)

        def end_of_tile(eng, r, tiles=T):
            eng.reg_mov(r["m"], -1)
            eng.reg_add(r["t"], r["t"], 1)
            with eng.If(eng.snap(r["t"]) >= tiles):
                eng.reg_mov(r["m"], -200)

        def in_last_item(eng, r):
            return eng.If(eng.snap(r["m"]) + 1 >= eng.snap(r["nm"]))

        def load_count(eng):
            def load(r):
                wait_alone(eng, (dve_fe, eng.snap(r["t"]) * 16 + 16))
                eng.reg_load(r["nm"], n_items[0:1, bass.ds(eng.snap(r["t"]), 1)])
            return load

        def mask_rows_of(parity):
            return mask_table[parity][0:N, :].rearrange("(p b) q -> p b q", p=P)

        @block.sync
        def _(sp):
            for i, w in enumerate((wq, wk, wv)):
                sp.dma_start(w_sb[i][:], w.rearrange("(a p) d -> p a d", p=P)).then_inc(ld_w, 16)
            sp.dma_start(we_sb[:].rearrange("p (h d) -> p h d", h=H),
                         we.unsqueeze(1).to_broadcast([P, H, HD])).then_inc(ld_c, 16)
            sp.dma_start(be_sb[:], be.unsqueeze(1).to_broadcast([P, 1])).then_inc(ld_c, 16)
            sp.dma_start(adj_in[:], adj[0:P, :]).then_inc(ld_adj, 16)
            sp.dma_start(x_row[:], x[0:P, :]).then_inc(ld_x0, 16)
            sp.wait_ge(dve_c, 1)
            sp.dma_start(kv_table[N:N + 1, :], zeros[0:1, :]).then_inc(st_c, 16)
            for i in range(TABLES):
                sp.dma_start(mask_table[i][N:N + 1, :], masked[:]).then_inc(st_c, 16)
            xg = x.rearrange("(g j p) d -> g p j d", j=GT, p=P)
            qg = q_table.rearrange("(g j) s d (i a) q -> g s (d i) j (a q)", j=GT, a=HALVES)
            kvg = kv_table[0:N, :].rearrange("(t p) r -> t p r", p=P)
            def load_q(tile):
                for i in range(PARTS):
                    sp.dma_start(q_next[HD * i:HD * i + HD], q_table[tile].rearrange("s d h q -> d s h q")
                                 ).then_inc(ld_q, 16)

            sp.dma_start(x_in[0][:], xg[0]).then_inc(ld_x[0], 16)

            def store_rows(g):
                for s in range(PARTS):
                    sp.wait_ge((q_hi, q_mid, q_low)[s], g * 2 + 2)
                    sp.dma_start(qg[g][s], q_out[s][:].rearrange("p j a q -> p j (a q)")).then_inc(st_q, 16)
                for j in range(GT):
                    sp.wait_ge(kv_low, g * GT + (j + 1))
                    sp.dma_start(kvg[g * GT + j], kv_out[j % 2][:]).then_inc(st_kv[j % 2], 16)

            def load_adj(f):
                sp.wait_ge(act_cast, f * 8)
                sp.dma_start(adj_in[:], adj[f * P:(f + 1) * P, :]).then_inc(ld_adj, 16)

            load_adj(1)
            with sp.Fori(0, G // 2 - 1) as gg:
                for odd in range(2):
                    sp.wait_ge(pe_xt, gg * 16 + 8 * odd)
                    sp.dma_start(x_in[1 - odd][:], xg[gg * 2 + (odd + 1)]).then_inc(ld_x[1 - odd], 16)
                    store_rows(gg * 2 + odd)
            sp.wait_ge(pe_xt, 8 * (G - 2))
            sp.dma_start(x_in[1][:], xg[G - 1]).then_inc(ld_x[1], 16)
            store_rows(G - 2)
            store_rows(G - 1)
            for f in range(2):
                sp.wait_ge(act_jt, f * 8 + 8)
                sp.dma_start(mask_rows_of(f), joined_t[:]).then_inc(st_mask, 16)
                load_adj(f + 2)
            sp.wait_ge(st_q, 16 * PARTS * G)
            load_q(0)

            def tile(t, place):
                last = T - TABLES + place if isinstance(t, int) else None
                if last is None or last + 1 < T:
                    sp.wait_ge(q_ready, t + 1)
                    load_q(t + 1)
                if last is None or last + 2 < T:
                    sp.wait_ge(act_jt, t * 8 + 24)
                    sp.dma_start(mask_rows_of((place + 2) % TABLES), joined_t[:]).then_inc(st_mask, 16)
                if last is None or last + 4 < T:
                    sp.wait_ge(act_cast, t * 8 + 32)
                    sp.dma_start(adj_in[:], adj[bass.ds(t * P + 4 * P, P), :]).then_inc(ld_adj, 16)
                if last is None or last + 1 < T:
                    sp.wait_ge(dve_ln, t * 8 + 9)
                    sp.dma_start(x_row[:], x[bass.ds(t * P + P, P), :]).then_inc(ld_x0, 16)
                sp.wait_ge(dve_ln, t * 8 + 16)
                sp.dma_start(out[bass.ds(t * P, P), :], y_out[:]).then_inc(st_out, 16)

            with sp.Fori(0, T // TABLES - 1) as four:
                for place in range(TABLES):
                    tile(four * TABLES + place, place)
            for place in range(TABLES):
                tile(T - TABLES + place, place)
            sp.wait_ge(st_out, 16 * (T + 1))
            sp.wait_ge(st_mask, 16 * T)
            sp.wait_ge(ld_q, QLOAD * T)

        @block.gpsimd
        def _(pool):
            pool.wait_ge(dve_c, 3)
            pool.affine_select(out=ident_f[:], in_=ident_f[:], compare_op=ALU.is_equal, fill=0.0, base=0,
                               pattern=[[-1, P]], channel_multiplier=1).then_inc(pool_c, 1)
            pool.affine_select(out=before[:], in_=before[:], compare_op=ALU.is_gt, fill=0.0, base=0,
                               pattern=[[1, P]], channel_multiplier=-1).then_inc(pool_c, 1)
            pool.iota(iota_chunk[:], [[1, NB]], base=0, channel_multiplier=0).then_inc(pool_c, 1)
            pool.iota(iota_slot[:], [[1, P]], base=0, channel_multiplier=0).then_inc(pool_c, 1)
            pool.iota(slot_id[:], [[P, NB]], base=0, channel_multiplier=1).then_inc(pool_c, 1)
            pool.iota(key_c[:], [[1, NB]], base=-N // 2, channel_multiplier=NB).then_inc(pool_c, 1)
            pool.wait_ge(st_c, 16 + 16 * TABLES)
            for i in range(2):
                pool.wait_ge(st_kv[i], 16 * T // 2)

            def item(b, first, r, it):
                n8, t = pool.snap(r["n8"]), pool.snap(r["t"])
                pool.reg_mov(r["off"], (t & (TABLES - 1)) * NB + pool.snap(r["m"]) * CHUNKS)
                off = pool.snap(r["off"])
                wait_alone(pool, (pe_pv, n8 + (A_PV - 16)))
                pool.tensor_copy(picks[b][:], lists[:, bass.ds(off, CHUNKS)]).then_inc(picked, 8)
                wait_alone(pool, (picked, n8 + 8))
                for c in range(CHUNKS):
                    pool.indirect_dma_start(kv[b][:, c, :], None, kv_table,
                                            bass.IndirectOffsetOnAxis(ap=picks[b][:, c:c + 1], axis=0)
                                            ).then_inc(landed[b], 16)
                def mask_gather(i):
                    for c in range(CHUNKS):
                        pool.indirect_dma_start(mrow[b][:, c, :], None, mask_table[i],
                                                bass.IndirectOffsetOnAxis(ap=picks[b][:, c:c + 1], axis=0)
                                                ).then_inc(landed[b], 16)
                for upper in range(2):
                    middle = pool.snap(r["off"]) < 2 * NB if upper == 0 else pool.snap(r["off"]) >= 2 * NB
                    with pool.If(middle):
                        for i in (2 * upper, 2 * upper + 1):
                            edge = (2 * upper + 1) * NB
                            with pool.If(pool.snap(r["off"]) < edge if i % 2 == 0 else pool.snap(r["off"]) >= edge):
                                mask_gather(i)
                with in_last_item(pool, r):
                    pool.sem_inc(lists_read, 1)
                    end_of_tile(pool, r, T + 1)

            def inner(r):
                with pool.If(pool.snap(r["t"]) < T):
                    load_count(pool)(r)
                    wait_alone(pool, (st_mask, pool.snap(r["t"]) * 16 + 16))
                with pool.If(pool.snap(r["t"]) >= T):
                    pool.reg_mov(r["nm"], 1)
            pool.sem_inc(lists_read, TABLES - 1)
            run_items(pool, item, inner, tiles=T + 1)

        @block.scalar
        def _(act):
            act.wait_ge(dve_c, 1)
            act.activation(std[:], eps[:], ACT.Sqrt)
            act.wait_ge(ld_adj, 16)
            act.activation(joined[:], adj_in[:], ACT.Sign, bias=minus_half[:]).then_inc(act_cast, 8)
            with act.Fori(0, G) as g:
                act.wait_ge(pe_xt, g * 8 + 8)
                act.copy(x_t[:, 0, :], ps_k[:]).then_inc(xt_copied, 4)
                act.wait_ge(st_q, g * (16 * PARTS))
                for a in range(HALVES):
                    act.wait_ge(pe_q, g * 8 + 4 * a + 4)
                    act.copy(q_out[0][:, :, a, :], ps_o[a][:].rearrange("p (j q) -> p j q", j=GT)
                             ).then_inc(q_hi, 1)
                for a in range(HALVES):
                    act.wait_ge(q_rested, g * 2 + (a + 1))
                    act.copy(q_out[1][:, :, a, :], q_rest[a][:].rearrange("p (j q) -> p j q", j=GT)
                             ).then_inc(q_mid, 1)

                def value_and_high(j):
                    act.wait_ge(pe_v, g * GT + (j + 1))
                    act.wait_ge(kv_rested, g * GT + (j - 1) if j else g * GT)
                    act.wait_ge(st_kv[j % 2], g * (16 * GT // 2) + 16 * (j // 2))
                    act.copy(kv_f[j % 2][:, D:2 * D], ps_t[j % 2][:, 0:D]).then_inc(v_copied, 1)
                    act.wait_ge(v_copied, g * GT + (j + 1))
                    act.wait_ge(k_done, g * GT + (j + 1))
                    act.copy(head_rows(kv_out[j % 2], HIGH), heads(kv_f[j % 2])).then_inc(kv_hi, 1)

                def middle(j):
                    act.wait_ge(kv_rested, g * GT + (j + 1))
                    act.copy(head_rows(kv_out[j % 2], MID), heads(kv_rest[j % 2])).then_inc(kv_mid, 1)

                value_and_high(0)
                for j in range(1, GT):
                    if j == 1:
                        value_and_high(1)
                        middle(0)
                    else:
                        value_and_high(j)
                        middle(j - 1)
                middle(GT - 1)

            def fe_cast(f8, f16):
                act.wait_ge(ld_adj, f16 + 16)
                act.wait_ge(pe_cnt, f8)
                act.activation(joined[:], adj_in[:], ACT.Sign, bias=minus_half[:]).then_inc(act_cast, 8)

            def joined_group(f8, g):
                act.wait_ge(pe_jt, f8 + 2 * g + 2)
                act.activation(joined_t[:, 8 * g:8 * g + 8, :].rearrange("p b q -> p (b q)"), as_bf16(ps_fe),
                               ACT.Copy, bias=-0.5, scale=0.5).then_inc(act_jt, 2)

            def row_std(l8):
                act.wait_ge(dve_ln, l8 + 3)
                act.activation(std[:], mean_var[:, 1:2], ACT.Sqrt, bias=eps[:]).then_inc(act_std, 8)

            def k_pair(next8, nb, p):
                act.wait_ge(pe_kt, next8 + (2 * p + 2))
                act.copy(k_t[nb][:, 2 * p:2 * p + 2, :].rearrange("p h k -> p (h k)"), as_bf16(ps_k)[0:HP, :]
                         ).then_inc(act_kt, 2)

            def mask_of(next8, nb):
                act.wait_ge(pe_mask, next8 + 8)
                act.activation(mask[nb][:], ps_k[:], ACT.Identity, bias=be_sb[:]).then_inc(act_mask, 8)

            act.wait_ge(ld_c, 32)
            for f in range(2):
                if f > 0:
                    act.wait_ge(st_mask, 16 * f)
                for g in range(4):
                    joined_group(8 * f, g)
                fe_cast(8 * f + 8, 16 * f + 16)
            mask_of(0, 0)
            for p in range(PAIRS):
                k_pair(0, 0, p)

            def item(b, first, r, it):
                n8, t = act.snap(r["n8"]), act.snap(r["t"])
                next8 = n8 + 8
                nb = (b + 1) % RING
                f8 = t * 8 + 16

                def next_cast():
                    with act.If(act.snap(r["t"]) < T - 3):
                        fe_cast(t * 8 + 24, t * 16 + 48)

                def pair(p):
                    act.wait_ge(pe_hard_t, n8 + (2 * p + 2 + A_HT))
                    act.wait_ge(pe_pv, n8 + (2 * p - 2 + A_PV))
                    act.copy(hard_t[p % 2][:], as_bf16(ps_t[p % 2])).then_inc(act_hard_t, 2)

                def next_k(p):
                    if first:
                        with act.If(act.snap(r["nm"]) > 1):
                            k_pair(next8, nb, p)
                    else:
                        k_pair(next8, nb, p)

                if first:
                    with act.If(act.snap(r["nm"]) > 1):
                        mask_of(next8, nb)
                    pair(0)
                    next_k(0)
                    pair(1)
                    next_k(1)
                    row_std(t * 8)
                    with act.If(t < T - 2):
                        act.wait_ge(st_mask, t * 16 + 32)
                        joined_group(f8, 0)
                    pair(2)
                    next_k(2)
                    with act.If(t < T - 2):
                        joined_group(f8, 1)
                    next_k(3)
                    with act.If(t < T - 2):
                        joined_group(f8, 2)
                    pair(3)
                    with act.If(t < T - 2):
                        joined_group(f8, 3)
                    with act.If(act.snap(r["nm"]) < 2):
                        mask_of(next8, nb)
                        for p in range(PAIRS):
                            k_pair(next8, nb, p)
                        next_cast()
                        end_of_tile(act, r)
                else:
                    mask_of(next8, nb)
                    for p in range(PAIRS - 1):
                        pair(p)
                        next_k(p)
                    next_k(3)
                    pair(3)
                    with in_last_item(act, r):
                        next_cast()
                        end_of_tile(act, r)

            run_items(act, item, load_count(act))
            row_std(8 * T)

        @block.vector
        def _(dve):
            dve.memset(zeros[:], 0.0)
            dve.memset(minus_half[:], -0.5)
            dve.memset(eps[:], EPS)
            dve.memset(mean_var[:], 0.0)
            dve.memset(hard_t[1][:], 0.0)
            dve.memset(kv[RING - 1][:, :, KW + 6 * HP:], 0.0)
            dve.memset(o_run[:], 0.0)
            dve.memset(keep[:], 0.0)
            dve.memset(ones_nb[:], 1.0)
            dve.memset(ones_b[:], 1.0)
            dve.memset(masked[:], -1.0).then_inc(dve_c, 1)
            dve.memset(ones_f[:], 1.0)
            dve.memset(before[:], 1.0).then_inc(dve_c, 1)
            dve.memset(ident_f[:], 1.0).then_inc(dve_c, 1)
            dve.wait_ge(pool_c, 6)
            dve.tensor_copy(iota_chunk_h[:], iota_chunk[:])
            dve.tensor_copy(iota_slot_h[:], iota_slot[:])
            dve.tensor_copy(key_h[:], key_c[:])
            dve.tensor_copy(ident_b[:], ident_f[:]).then_inc(dve_c, 1)
            dve.tensor_scalar(ident_big[:], ident_f[:], BIG, None, ALU.mult).then_inc(dve_c, 1)
            for i in range(3):
                dve.wait_ge(pe_w, i + 1)
                if i == 0:
                    for c in range(HALVES):
                        done = dve.tensor_copy(
                            w_t[0][:, c, :].rearrange("p (a d i) -> p a d i", a=HALVES, d=HD),
                            ps_s[0][:, c * D:c * D + D].rearrange("p (i a d) -> p a d i", a=HALVES, d=HD))
                    done.then_inc(dve_w, 1)
                else:
                    dve.tensor_copy(w_t[i][:].rearrange("p a e -> p (a e)"), (ps_s + ps_t)[i][:]).then_inc(dve_w, 1)
            dve.wait_ge(ld_c, 32)
            with dve.Fori(0, G) as g:
                dve.wait_ge(pe_xt, g * 8 + 8)
                dve.tensor_copy(x_t[:, 1, :], ps_fe[:]).then_inc(xt_copied, 4)
                for a in range(HALVES):
                    dve.wait_ge(q_hi, g * 2 + (a + 1))
                    dve.tensor_tensor(q_rest[a][:].rearrange("p (j q) -> p j q", j=GT),
                                      ps_o[a][:].rearrange("p (j q) -> p j q", j=GT), q_out[0][:, :, a, :],
                                      ALU.subtract).then_inc(q_rested, 1)
                for a in range(HALVES):
                    dve.wait_ge(q_mid, g * 2 + (a + 1))
                    dve.tensor_tensor(q_out[2][:, :, a, :], q_rest[a][:].rearrange("p (j q) -> p j q", j=GT),
                                      q_out[1][:, :, a, :], ALU.subtract).then_inc(q_low, 1)

                def k_and_rest(j):
                    dve.wait_ge(pe_k, g * GT + (j + 1))
                    dve.wait_ge(kv_hi, g * GT + (j - 1) if j else g * GT)
                    dve.scalar_tensor_tensor(out=kv_f[j % 2][:, 0:D], in0=ps_s[j % 2][:, 0:D], scalar=SCALE,
                                             in1=we_sb[:], op0=ALU.mult, op1=ALU.add).then_inc(k_done, 1)
                    dve.wait_ge(kv_hi, g * GT + (j + 1))
                    dve.wait_ge(kv_low, g * GT + (j - 1) if j else g * GT)
                    dve.tensor_tensor(heads(kv_rest[j % 2]), heads(kv_f[j % 2]), head_rows(kv_out[j % 2], HIGH),
                                      ALU.subtract).then_inc(kv_rested, 1)

                def low(j):
                    dve.wait_ge(kv_mid, g * GT + (j + 1))
                    dve.tensor_tensor(head_rows(kv_out[j % 2], LOW), heads(kv_rest[j % 2]),
                                      head_rows(kv_out[j % 2], MID), ALU.subtract).then_inc(kv_low, 1)

                k_and_rest(0)
                for j in range(1, GT):
                    k_and_rest(j)
                    low(j - 1)
                low(GT - 1)

            def fe_scan(f8, f16):
                dve.wait_ge(pe_cnt, f8 + 8)
                dve.tensor_scalar(flag[:], ps_fe[:, 0:NB], 1.0 - P, None, ALU.is_gt).then_inc(dve_fe, 1)
                dve.wait_ge(dve_fe, f16 + 1)
                dve.tensor_tensor_scan(prefix[:], ones_nb[:], flag[:], 0.0, ALU.mult, ALU.add).then_inc(dve_fe, 1)

            def fe_hot(f8, f16, f):
                dve.wait_ge(pe_base, f8 + 8)
                dve.scalar_tensor_tensor(out=rank1[:], in0=prefix[:], scalar=ps_fe[:, 64:65], in1=flag[:],
                                         op0=ALU.add, op1=ALU.mult).then_inc(dve_fe, 1)
                dve.wait_ge(dve_fe, f16 + 3)
                dve.tensor_scalar(rank[:], rank1[:], -1.0, None, ALU.add).then_inc(dve_fe, 1)
                dve.wait_ge(dve_fe, f16 + 4)
                dve.tensor_scalar(digits[:, 0], rank[:], 7, None, ALU.arith_shift_right)
                dve.tensor_scalar(digits[:, 1], rank[:], 127, None, ALU.bitwise_and).then_inc(dve_fe, 1)
                dve.wait_ge(dve_fe, f16 + 5)
                dve.tensor_copy(digits_h[:], digits[:]).then_inc(dve_fe, 1)
                dve.wait_ge(dve_fe, f16 + 6)
                dve.tensor_tensor(hot_hi[:], digits_h[:, 0].unsqueeze(2).to_broadcast([P, NB, NB]),
                                  iota_chunk_h[:].unsqueeze(1).to_broadcast([P, NB, NB]),
                                  ALU.is_equal).then_inc(dve_fe, 1)
                dve.tensor_tensor(hot_lo[:], digits_h[:, 1].unsqueeze(2).to_broadcast([P, NB, P]),
                                  iota_slot_h[:].unsqueeze(1).to_broadcast([P, NB, P]),
                                  ALU.is_equal).then_inc(dve_fe, 1)
                dve.wait_ge(dve_fe, f16 + 7)
                dve.tensor_tensor(hot_key[:], hot_hi[:], key_h[:].unsqueeze(2).to_broadcast([P, NB, NB]),
                                  ALU.mult).then_inc(dve_fe, 1)
                dve.tensor_scalar(total_i[:], ps_fe[:, 65:66], float(SLOTS - 1), None, ALU.add).then_inc(dve_fe, 1)
                dve.wait_ge(dve_fe, f16 + 10)
                dve.tensor_scalar(n_items[:, bass.ds(f, 1)], total_i[:], 9, None, ALU.arith_shift_right).then_inc(dve_fe, 1)

                dve.tensor_scalar(unused[:], slot_id[:], ps_fe[:, 65:66], float(N), ALU.is_ge,
                                  ALU.mult).then_inc(dve_fe, 1)

            def fe_list(f8, f16, f):
                dve.wait_ge(dve_fe, f16 + 12)
                dve.wait_ge(pe_list, f8 + 8)
                dve.scalar_tensor_tensor(out=list_f[:], in0=ps_fe[:, 128:128 + NB], scalar=float(N // 2),
                                         in1=unused[:], op0=ALU.add, op1=ALU.max).then_inc(dve_fe, 1)
                dve.wait_ge(dve_fe, f16 + 13)
                dve.wait_ge(lists_read, f)
                off = (f % TABLES if isinstance(f, int) else f & (TABLES - 1)) * NB
                dve.tensor_copy(lists[:, bass.ds(off, NB)], list_f[:]).then_inc(dve_fe, 3)

            fe_scan(0, 0)
            fe_hot(0, 0, 0)
            fe_list(0, 0, 0)
            fe_scan(8, 16)
            fe_hot(8, 16, 1)

            def merge(n8):
                for k in range(2):
                    dve.wait_ge(pe_pv, n8 + (4 * k + 4 - 8 + A_PV))
                    dve.tensor_reduce(o_item[:, 4 * k:4 * k + 4, :],
                                      ps_o[k][:, 0:4 * PARTS * HD].rearrange("p (h s d) -> p h d s", h=4, s=PARTS),
                                      AX.X, ALU.add).then_inc(dve_osum, 4)
                dve.wait_ge(dve_merge, n8)
                dve.wait_ge(dve_keep, n8)
                dve.tensor_tensor(o_run[:], o_run[:], keep[:].unsqueeze(2).to_broadcast([P, H, HD]),
                                  ALU.mult).then_inc(dve_merge, 4)
                dve.wait_ge(dve_osum, n8 + 8)
                dve.wait_ge(dve_merge, n8 + 4)
                dve.tensor_tensor(o_run[:], o_run[:], o_item[:], ALU.add).then_inc(dve_merge, 4)

            def norm_stats(l8, l16, n8):
                dve.wait_ge(ld_x0, l16)
                dve.wait_ge(dve_merge, n8 + 8)
                dve.scalar_tensor_tensor(out=y[:], in0=o_run[:].rearrange("p h d -> p (h d)"), scalar=1.0 / H,
                                         in1=x_row[:], op0=ALU.mult, op1=ALU.add).then_inc(dve_ln, 1)
                dve.wait_ge(dve_ln, l8 + 1)
                dve.bn_stats(stats[:], y[:]).then_inc(dve_ln, 1)
                wait_alone(dve, (dve_ln, l8 + 2)) if not isinstance(l8, int) else dve.wait_ge(dve_ln, l8 + 2)
                dve.bn_aggr(mean_var[:], stats[:]).then_inc(dve_ln, 1)

            def norm_apply(l8, l16):
                dve.wait_ge(act_std, l8 + 8)
                dve.reciprocal(rstd[:], std[:]).then_inc(dve_ln, 1)
                dve.wait_ge(dve_ln, l8 + 4)
                dve.wait_ge(st_out, l16)
                dve.tensor_scalar(y_out[:], y[:], mean_var[:, 0:1], rstd[:, 0:1], ALU.subtract,
                                  ALU.mult).then_inc(dve_ln, 4)

            def take_q(landed_tiles, scores_done):
                dve.wait_ge(ld_q, landed_tiles)
                dve.wait_ge(pe_score, scores_done)
                dve.tensor_copy(q_cur[:].rearrange("p s h q -> p (s h q)"),
                                q_next[:].rearrange("p s h q -> p (s h q)")).then_inc(q_ready, 1)

            take_q(QLOAD, 0)
            dve.sem_inc(dve_top, A_TOP)
            dve.sem_inc(dve_ln, 8)
            dve.sem_inc(st_out, 16)

            def item(b, first, r, it):
                n8, t = dve.snap(r["n8"]), dve.snap(r["t"])
                nb = (b + 1) % RING
                f8, f16 = t * 8 + 16, t * 16 + 32

                def tops(p):
                    for h in (2 * p, 2 * p + 1):
                        wait_alone(dve, (pe_score, n8 + (h + 1)), *[(act_mask, n8 + 8)][:h == 0])
                        dve.tensor_tensor_reduce(out=score[h % 4][:], in0=ps_s[h % 2][:], in1=mask[b][:], scale=1.0,
                                                 scalar=FLOOR if first else top[b - 1][:, h:h + 1], op0=ALU.add, op1=ALU.max,
                                                 accum_out=top[b][:, h:h + 1]).then_inc(dve_top, 1)

                def hards(p):
                    dve.wait_ge(pe_hard_t, n8 + (2 * p - 2 + A_HT))
                    for h in (2 * p, 2 * p + 1):
                        dve.wait_ge(dve_top, n8 + (h + 1 + A_TOP))
                        dve.tensor_scalar(hard[h % 4][:], score[h % 4][:], top[b][:, h:h + 1], None,
                                          ALU.is_equal).then_inc(dve_hard, 1)

                if not first:
                    wait_alone(dve, (dve_top, n8 + A_TOP))
                for p in range(4):
                    tops(p)
                    hards(p)
                    if p == 0:
                        if first:
                            with dve.If(t < T - 1):
                                fe_list(t * 8 + 8, t * 16 + 16, t + 1)
                        else:
                            with in_last_item(dve, r):
                                with dve.If(t < T - 2):
                                    fe_scan(f8, f16)
                    if p == 1:
                        merge(n8)
                        if first:
                            with dve.If(t > 0):
                                norm_stats(t * 8, t * 16, n8)
                    if p == 2 and first:
                        with dve.If(t > 0):
                            norm_apply(t * 8, t * 16)
                dve.wait_ge(dve_merge, n8 + 8)
                if first:
                    dve.memset(keep[:], 0.0).then_inc(dve_keep, 8)
                    with dve.If(dve.snap(r["nm"]) < 2):
                        with dve.If(t < T - 2):
                            fe_scan(f8, f16)
                            fe_hot(f8, f16, t + 2)
                        with dve.If(t < T - 1):
                            take_q(t * QLOAD + 2 * QLOAD, n8 + 8)
                        end_of_tile(dve, r)
                else:
                    dve.wait_ge(dve_top, n8 + (8 + A_TOP))
                    dve.tensor_tensor(keep[:], top[b - 1][:], top[b][:], ALU.is_equal).then_inc(dve_keep, 8)
                    with in_last_item(dve, r):
                        with dve.If(t < T - 1):
                            take_q(t * QLOAD + 2 * QLOAD, n8 + 8)
                        with dve.If(t < T - 2):
                            fe_hot(f8, f16, t + 2)
                        end_of_tile(dve, r)

            def closing(b, n8):
                merge(n8)
                norm_stats(8 * T, 16 * T, n8)
                norm_apply(8 * T, 16 * T)
            run_items(dve, item, load_count(dve), closing=closing)

        @block.tensor
        def _(pe):
            pe.wait_ge(pool_c, 6)
            pe.wait_ge(dve_c, 5)
            for k in range(2):
                mm = pe.matmul(ps_o[k][:, 0:384], ident_b[:], zeros[:, 0:384], start=True, stop=True)
            mm.then_inc(pe_pv, A_PV - 2)
            pe.wait_ge(ld_w, 48)
            for i in range(3):
                for a in range(HALVES):
                    for c in range(HALVES):
                        mm = pe.transpose((ps_s + ps_t)[i][:, c * D + a * P:c * D + a * P + P],
                                          w_sb[i][:, a, c * P:c * P + P], ident_f[:])
                mm.then_inc(pe_w, 1)
            pe.wait_ge(dve_w, 3)
            pe.wait_ge(pe_pv, A_PV - 2)
            with pe.Fori(0, G // 2) as gg:
                for odd in range(2):
                    g = gg * 2 + odd
                    pe.wait_ge(ld_x[odd], gg * 16 + 16)
                    pe.wait_ge(xt_copied, g * 8)
                    for c, bank in enumerate((ps_k, ps_fe)):
                        for j in range(GT):
                            mm = pe.transpose(bank[:, j * P:j * P + P], x_in[odd][:, j, c * P:c * P + P], ident_f[:])
                    mm.then_inc(pe_xt, 8)
                    pe.wait_ge(xt_copied, g * 8 + 8)
                    pe.wait_ge(q_rested, g * 2)
                    for a in range(HALVES):
                        for c in range(HALVES):
                            mm = pe.matmul(ps_o[a][:], w_t[0][:, c, a * P:a * P + P], x_t[:, c, :],
                                           start=(c == 0), stop=(c == 1))
                        mm.then_inc(pe_q, 4)
                    for j in range(GT):
                        if j < 2:
                            pe.wait_ge(k_done, g * GT)
                            pe.wait_ge(v_copied, g * GT)
                        else:
                            pe.wait_ge(k_done, g * GT + (j - 1))
                            pe.wait_ge(v_copied, g * GT + (j - 1))
                        for i, bank, done in ((1, ps_s, pe_k), (2, ps_t, pe_v)):
                            for c in range(HALVES):
                                mm = pe.matmul(bank[j % 2][:, 0:D], x_t[:, c, j * P:j * P + P], w_t[i][:, c, :],
                                               start=(c == 0), stop=(c == 1))
                            mm.then_inc(done, 1)

            blocks = joined[:].rearrange("q (p b) -> q b p", b=NB)

            def fe_transpose(f8, f16, g):
                if g == 0:
                    pe.wait_ge(act_cast, f8 + 8)
                    pe.wait_ge(dve_fe, f16)
                else:
                    pe.wait_ge(act_jt, f8 + 2 * g)
                for b in range(8):
                    mm = pe.transpose(as_bf16(ps_fe)[:, b * P:b * P + P], blocks[:, 8 * g + b, :], ident_b[:])
                mm.then_inc(pe_jt, 2)

            def fe_count(f8):
                pe.wait_ge(act_jt, f8 + 8)
                for b in range(NB):
                    mm = pe.matmul(ps_fe[:, b:b + 1], blocks[:, b, :], ones_b[:], start=True, stop=True)
                mm.then_inc(pe_cnt, 8)

            def fe_base(f8, f16):
                pe.wait_ge(dve_fe, f16 + 2)
                pe.matmul(ps_fe[:, 64:65], before[:], prefix[:, NB - 1:NB], start=True, stop=True)
                pe.matmul(ps_fe[:, 65:66], ones_f[:], prefix[:, NB - 1:NB], start=True,
                          stop=True).then_inc(pe_base, 8)

            def fe_list(f8, f16):
                pe.wait_ge(dve_fe, f16 + 12)
                for b in range(NB):
                    mm = pe.matmul(ps_fe[:, 128:128 + NB], hot_lo[:, b, :], hot_key[:, b, :], start=(b == 0),
                                   stop=(b == NB - 1))
                mm.then_inc(pe_list, 8)

            def k_pair(n8, nb, p):
                if p == 0:
                    pe.wait_ge(act_mask, n8 + 8)
                else:
                    pe.wait_ge(act_kt, n8 + 2 * p)
                for h in (2 * p, 2 * p + 1):
                    for c in range(CHUNKS):
                        at = (h % 2) * SLOTS + c * P
                        mm = pe.transpose(as_bf16(ps_k)[0:HP, at:at + P],
                                          kv[nb][:, c, h * HP:(h + 1) * HP], ident_b[:])
                mm.then_inc(pe_kt, 2)

            def mask_rows(n8, nb, uses):
                pe.wait_ge(landed[nb], uses)
                pe.wait_ge(act_kt, n8)
                for c in range(CHUNKS):
                    mm = pe.matmul(ps_k[:, c * P:c * P + P], mrow[nb][:, c, :], ident_big[:], start=True, stop=True)
                mm.then_inc(pe_mask, 8)

            def scores(n8, b, h):
                pe.wait_ge(dve_top, n8 + (h - 1 + A_TOP))
                if h % 2 == 0:
                    pe.wait_ge(act_kt, n8 + (h + 2))
                for i in range(PARTS):
                    mm = pe.matmul(ps_s[h % 2][:], q_cur[:, i, h, :], k_t[b][:, h, :], start=(i == 0),
                                   stop=(i == PARTS - 1))
                mm.then_inc(pe_score, 1)

            def values(n8, b, p):
                at8 = n8 + 8
                pe.wait_ge(act_hard_t, at8 + (2 * p + 2 + A_HC - 8))
                if p % 2 == 0:
                    pe.wait_ge(dve_osum, at8 + (2 * p + 4 - 8))
                for h in (2 * p, 2 * p + 1):
                    for c in range(CHUNKS):
                        at = (h % 2) * SLOTS + c * P
                        mm = pe.matmul(ps_o[h // 4][:, (h % 4) * HP:(h % 4 + 1) * HP],
                                       hard_t[p % 2][:, at:at + P],
                                       kv[b][:, c, KW + h * HP:KW + (h + 1) * HP],
                                       start=(c == 0), stop=(c == CHUNKS - 1))
                mm.then_inc(pe_pv, 2)

            for f in range(2):
                for g in range(4):
                    fe_transpose(8 * f, 16 * f, g)
                fe_count(8 * f)
                fe_base(8 * f, 16 * f)
                if f == 0:
                    fe_list(0, 0)
            mask_rows(0, 0, 128)
            for p in range(PAIRS):
                k_pair(0, 0, p)
            pe.sem_inc(pe_hard_t, A_HT)
            pe.sem_inc(act_hard_t, A_HC)
            pe.wait_ge(q_ready, 1)
            scores(0, 0, 0)
            scores(0, 0, 1)

            def item(b, first, r, it):
                n8, t = pe.snap(r["n8"]), pe.snap(r["t"])
                next8 = n8 + 8
                nb = (b + 1) % RING
                uses = it * 128 + (128 if b < RING - 1 else 256)
                f8, f16 = t * 8 + 16, t * 16 + 32

                def transposes(p):
                    pe.wait_ge(dve_hard, n8 + (2 * p + 2))
                    pe.wait_ge(act_hard_t, n8 + (2 * p - 2 + A_HC))
                    for h in (2 * p, 2 * p + 1):
                        for c in range(CHUNKS):
                            at = (h % 2) * SLOTS + c * P
                            mm = pe.transpose(as_bf16(ps_t[p % 2])[:, at:at + P], hard[h % 4][:, c * P:c * P + P],
                                              ident_b[:])
                    mm.then_inc(pe_hard_t, 2)

                def next_tile_q():
                    with pe.If(pe.snap(r["t"]) < T):
                        pe.wait_ge(q_ready, pe.snap(r["t"]) + 1)

                def next_k(p):
                    if first:
                        with pe.If(pe.snap(r["nm"]) > 1):
                            k_pair(next8, nb, p)
                    else:
                        k_pair(next8, nb, p)

                def front_end(before, stage):
                    if first:
                        with pe.If(t < before):
                            stage()

                def in_last(stage):
                    if not first:
                        with in_last_item(pe, r):
                            with pe.If(t < T - 2):
                                stage()

                scores(n8, b, 2)
                scores(n8, b, 3)
                values(n8 - 8, (b - 1) % RING, 3)
                front_end(T - 1, lambda: fe_list(t * 8 + 8, t * 16 + 16))
                in_last(lambda: fe_count(f8))
                if first:
                    with pe.If(pe.snap(r["nm"]) > 1):
                        mask_rows(next8, nb, uses)
                else:
                    mask_rows(next8, nb, uses)
                transposes(0)
                next_k(0)
                scores(n8, b, 4)
                scores(n8, b, 5)
                transposes(1)
                next_k(1)
                values(n8, b, 0)
                front_end(T - 2, lambda: fe_transpose(f8, f16, 0))
                in_last(lambda: fe_base(f8, f16))
                scores(n8, b, 6)
                scores(n8, b, 7)
                transposes(2)
                next_k(2)
                front_end(T - 2, lambda: fe_transpose(f8, f16, 1))
                if first:
                    with pe.If(pe.snap(r["nm"]) > 1):
                        scores(next8, nb, 0)
                        scores(next8, nb, 1)
                else:
                    with in_last_item(pe, r):
                        end_of_tile(pe, r)
                        next_tile_q()
                    scores(next8, nb, 0)
                    scores(next8, nb, 1)
                values(n8, b, 1)
                next_k(3)
                front_end(T - 2, lambda: fe_transpose(f8, f16, 2))
                transposes(3)
                values(n8, b, 2)
                front_end(T - 2, lambda: fe_transpose(f8, f16, 3))
                if first:
                    with pe.If(pe.snap(r["nm"]) < 2):
                        with pe.If(t < T - 2):
                            fe_count(f8)
                            fe_base(f8, f16)
                        mask_rows(next8, nb, uses)
                        for p in range(PAIRS):
                            k_pair(next8, nb, p)
                        end_of_tile(pe, r)
                        next_tile_q()
                        scores(next8, nb, 0)
                        scores(next8, nb, 1)

            run_items(pe, item, load_count(pe), closing=lambda b, n8: values(n8 - 8, (b - 1) % RING, 3))


_INS = ["x", "adj", "L0_gnn_WQ", "L0_gnn_WK", "L0_gnn_WV", "L0_gnn_we", "L0_gnn_be"]


def kernel(**inputs):
    import numpy as np
    import concourse.bacc as bacc
    from concourse.bass_utils import run_bass_kernel_spmd

    nc = bacc.Bacc("TRN2", target_bir_lowering=False, num_devices=1)
    arrays, args = {}, []
    for name in _INS:
        a = np.ascontiguousarray(inputs[name])
        arrays[f"in_{name}"] = a
        args.append(nc.dram_tensor(f"in_{name}", a.shape, mybir.dt.from_np(a.dtype), kind="ExternalInput").ap())
    args.append(nc.dram_tensor("out_0", inputs["x"].shape, mybir.dt.float32, kind="ExternalOutput").ap())
    hard_attention(nc, *args)
    r = run_bass_kernel_spmd(nc, [arrays], core_ids=[0])
    return r.results[0]["out_0"]
```

```python
from contextlib import ExitStack

import concourse.bass as bass
from concourse import mybir

ALU = mybir.AluOpType
ACT = mybir.ActivationFunctionType
AX = mybir.AxisListType
F32 = mybir.dt.float32
BF16 = mybir.dt.bfloat16
F16 = mybir.dt.float16
I32 = mybir.dt.int32
U32 = mybir.dt.uint32

P = 128
HD = 32
PARTS = 3
CHUNKS = 4
SLOTS = CHUNKS * P
RING = 3
TABLES = 4
EPS = 1e-5
BIG = 2.0 ** 100
FLOOR = -(2.0 ** 90)


def hard_attention(nc, x, adj, wq, wk, wv, we, be, out):
    N, D = x.shape
    H = D // HD
    T = N // P
    NB = N // P
    HALVES = D // P
    PAIRS = H // 2
    HP = PARTS * HD
    KW = H * HP
    ROW = 2 * KW
    TURNS_INNER = 8
    TURNS_OUTER = -(-(T * (N // SLOTS) + 2) // (RING * TURNS_INNER))
    GT = 4
    G = T // GT
    SCALE = float(HD) ** -0.5
    assert D == 256 and N == 4096 and SLOTS == 512 and H == 8

    kv_table = nc.dram_tensor("kv_table", (N + 1, ROW), BF16, kind="Internal").ap()
    mask_table = [nc.dram_tensor(f"mask_table{i}", (N + 1, P), BF16, kind="Internal").ap() for i in range(TABLES)]
    q_table = nc.dram_tensor("q_table", (T, PARTS, HD, H, P), BF16, kind="Internal").ap()

    with ExitStack() as ctx:
        def sb(name, shape, dt):
            return ctx.enter_context(nc.sbuf_tensor(name, shape, dt))

        def pb(name, dt=F32):
            return ctx.enter_context(nc.psum_tensor(name, [P, 512], dt))

        def sem(name):
            return ctx.enter_context(nc.semaphore(name))

        ident_f = sb("ident_f", [P, P], F32)
        ident_b = sb("ident_b", [P, P], BF16)
        ident_big = sb("ident_big", [P, P], BF16)
        before = sb("before", [P, P], F32)
        ones_f = sb("ones_f", [P, P], F32)
        ones_b = sb("ones_b", [P, 1], BF16)
        iota_chunk = sb("iota_chunk", [P, NB], I32)
        iota_slot = sb("iota_slot", [P, P], I32)
        slot_id = sb("slot_id", [P, NB], I32)
        key_c = sb("key_c", [P, NB], I32)
        iota_chunk_h = sb("iota_chunk_h", [P, NB], F16)
        iota_slot_h = sb("iota_slot_h", [P, P], F16)
        key_h = sb("key_h", [P, NB], F16)
        be_sb = sb("be_sb", [P, 1], F32)
        we_sb = sb("we_sb", [P, D], F32)
        zeros = sb("zeros", [P, ROW], BF16)
        minus_half = sb("minus_half", [P, 1], F32)
        eps = sb("eps", [P, 1], F32)
        masked = sb("masked", [1, P], BF16)
        w_sb = [sb(f"w{i}", [P, HALVES, D], F32) for i in range(3)]
        w_t = [sb(f"wt{i}", [P, HALVES, D], F32) for i in range(3)]
        x_in = [sb(f"x_in{i}", [P, GT, D], F32) for i in range(2)]
        x_t = [sb(f"x_t{i}", [P, HALVES, GT * P], F32) for i in range(2)]
        q_out = [sb(f"q_out{i}", [P, GT, HALVES, P], BF16) for i in range(PARTS)]
        kv_out = [sb(f"kv_out{i}", [P, ROW], BF16) for i in range(GT)]
        kv_f = [sb(f"kv_f{i}", [P, 2 * D], F32) for i in range(2)]
        adj_in = sb("adj_in", [P, N], I32)
        joined = sb("joined", [P, N], BF16)
        joined_t = sb("joined_t", [P, NB, P], BF16)
        flag = sb("flag", [P, NB], F32)
        ones_nb = sb("ones_nb", [P, NB], F32)
        prefix = sb("prefix", [P, NB], F32)
        rank1 = sb("rank1", [P, NB], F32)
        rank = sb("rank", [P, NB], I32)
        digits = sb("digits", [P, 2, NB], I32)
        digits_h = sb("digits_h", [P, 2, NB], F16)
        hot_hi = sb("hot_hi", [P, NB, NB], F16)
        hot_key = sb("hot_key", [P, NB, NB], F16)
        hot_lo = sb("hot_lo", [P, NB, P], F16)
        total_i = sb("total_i", [P, 1], I32)
        n_items = sb("n_items", [P, T], I32)
        unused = sb("unused", [P, NB], F32)
        list_f = sb("list_f", [P, NB], F32)
        lists = sb("lists", [P, TABLES * NB], U32)
        picks = [sb(f"picks{i}", [P, CHUNKS], U32) for i in range(RING)]
        kv = [sb(f"kv{i}", [P, CHUNKS, ROW], BF16) for i in range(RING)]
        mrow = [sb(f"mrow{i}", [P, CHUNKS, P], BF16) for i in range(RING)]
        k_t = [sb(f"k_t{i}", [HP, H, SLOTS], BF16) for i in range(RING)]
        mask = [sb(f"mask{i}", [P, SLOTS], F32) for i in range(RING)]
        q_next = sb("q_next", [HP, PARTS, H, P], BF16)
        q_cur = sb("q_cur", [HP, PARTS, H, P], BF16)
        score = [sb(f"score{i}", [P, SLOTS], F32) for i in range(4)]
        q_rest, kv_rest = score[0:2], score[2:4]
        hard = [sb(f"hard{i}", [P, SLOTS], BF16) for i in range(4)]
        hard_t = [sb(f"hard_t{i}", [P, 2 * SLOTS], BF16) for i in range(2)]
        top = [sb(f"top{i}", [P, H], F32) for i in range(RING)]
        keep = sb("keep", [P, H], F32)
        o_item = sb("o_item", [P, H, HD], F32)
        o_run = sb("o_run", [P, H, HD], F32)
        x_row = sb("x_row", [P, D], F32)
        y = sb("y", [P, D], F32)
        stats = sb("stats", [P, 6], F32)
        mean_var = sb("mean_var", [P, 2], F32)
        std = sb("std", [P, 1], F32)
        rstd = sb("rstd", [P, 1], F32)
        y_out = sb("y_out", [P, D], F32)

        ps_s = [pb("ps_s0"), pb("ps_s1")]
        ps_t = [pb("ps_t0"), pb("ps_t1")]
        ps_o = [pb("ps_o0"), pb("ps_o1")]
        ps_k = pb("ps_k")
        ps_fe = pb("ps_fe")

        def as_bf16(bank):
            return bank[:].bitcast(BF16)

        def heads(cols):
            return cols[:].rearrange("p (h d) -> p h d", d=HD)

        def head_rows(row, part):
            return row[:].rearrange("p (h s d) -> p h s d", s=PARTS, d=HD)[:, :, part, :]

        HIGH, MID, LOW = 0, 1, 2

        ld_w, ld_c, ld_x, ld_x0, ld_q = (
            sem("ld_w"), sem("ld_c"), [sem("ld_x_even"), sem("ld_x_odd")], sem("ld_x0"), sem("ld_q"))
        ld_adj = sem("ld_adj")
        pool_c, dve_c = sem("pool_c"), sem("dve_c")
        pe_w, dve_w = sem("pe_w"), sem("dve_w")
        pe_xt, xt_copied = sem("pe_xt"), sem("xt_copied")
        pe_q, st_q = sem("pe_q"), sem("st_q")
        q_hi, q_rested, q_mid, q_low = sem("q_hi"), sem("q_rested"), sem("q_mid"), sem("q_low")
        pe_k, pe_v, k_done, v_copied, kv_hi, kv_rested, kv_mid, kv_low = (
            sem("pe_k"), sem("pe_v"), sem("k_done"), sem("v_copied"), sem("kv_hi"), sem("kv_rested"),
            sem("kv_mid"), sem("kv_low"))
        st_kv = [sem(f"st_kv{j}") for j in range(GT)]
        st_c = sem("st_c")
        act_cast, pe_jt, act_jt, pe_cnt, dve_fe, pe_base, pe_list, st_mask, lists_read = (
            sem("act_cast"), sem("pe_jt"), sem("act_jt"), sem("pe_cnt"), sem("dve_fe"), sem("pe_base"),
            sem("pe_list"), sem("st_mask"), sem("lists_read"))
        picked = sem("picked")
        landed = [sem(f"landed{i}") for i in range(RING)]
        pe_kt, act_kt, pe_mask, act_mask = sem("pe_kt"), sem("act_kt"), sem("pe_mask"), sem("act_mask")
        pe_score, dve_top, dve_hard, pe_hard_t, act_hard_t, pe_pv = (
            sem("pe_score"), sem("dve_top"), sem("dve_hard"), sem("pe_hard_t"), sem("act_hard_t"), sem("pe_pv"))
        dve_osum, dve_merge, dve_keep, q_ready = sem("dve_osum"), sem("dve_merge"), sem("dve_keep"), sem("q_ready")
        dve_ln, act_std, st_out = sem("dve_ln"), sem("act_std"), sem("st_out")
        A_TOP, A_HT, A_HC, A_PV = 2, 4, 4, 16
        QLOAD = 16 * PARTS

        block = ctx.enter_context(nc.Block())

        scratch = {}

        def wait_alone(eng, *waits):
            regs = scratch.setdefault(str(eng.engine), [eng.alloc_register(f"wait{i}") for i in range(2)]
                                      if str(eng.engine) not in scratch else None)
            for (_, value), reg in zip(waits, regs):
                eng.reg_mov(reg, value)
            eng.wait_ge(dve_c, 1)
            for (waited, _), reg in zip(waits, regs):
                eng.wait_ge(waited, reg)

        def run_items(eng, item, inner, tiles=T, closing=None):
            r = {k: eng.alloc_register(k) for k in ("n8", "left", "nm", "t", "off")}
            for k in r:
                eng.reg_mov(r[k], 0)
            end = tiles + (closing is not None)
            with eng.Fori(0, TURNS_OUTER) as outer:
                with eng.If(eng.snap(r["t"]) < end):
                    with eng.Fori(0, TURNS_INNER) as turn:
                        with eng.If(eng.snap(r["t"]) < end):
                            for b in range(RING):
                                place(eng, item, inner, tiles, closing, b, r, outer * TURNS_INNER + turn)

        def place(eng, item, inner, tiles, closing, b, r, it):
            with eng.If(eng.snap(r["left"]) > 0):
                item(b, False, r, it)
            with eng.If(eng.snap(r["left"]) < 1):
                if closing is not None:
                    with eng.If(eng.snap(r["t"]) >= tiles):
                        with eng.If(eng.snap(r["t"]) < tiles + 1):
                            closing(b, eng.snap(r["n8"]))
                            eng.reg_add(r["t"], r["t"], 1)
                with eng.If(eng.snap(r["t"]) < tiles):
                    inner(r)
                    eng.reg_mov(r["left"], r["nm"])
                    item(b, True, r, it)
            eng.reg_add(r["n8"], r["n8"], 8)
            eng.reg_add(r["left"], r["left"], -1)

        def end_of_tile(eng, r):
            eng.reg_add(r["t"], r["t"], 1)

        def in_last_item(eng, r):
            return eng.If(eng.snap(r["left"]) < 2)

        def load_count(eng):
            def load(r):
                wait_alone(eng, (dve_fe, eng.snap(r["t"]) * 16 + 16))
                eng.reg_load(r["nm"], n_items[0:1, bass.ds(eng.snap(r["t"]), 1)])
            return load

        def mask_rows_of(parity):
            return mask_table[parity][0:N, :].rearrange("(p b) q -> p b q", p=P)

        @block.sync
        def _(sp):
            for i, w in enumerate((wq, wk, wv)):
                sp.dma_start(w_sb[i][:], w.rearrange("(a p) d -> p a d", p=P)).then_inc(ld_w, 16)
            sp.dma_start(we_sb[:].rearrange("p (h d) -> p h d", h=H),
                         we.unsqueeze(1).to_broadcast([P, H, HD])).then_inc(ld_c, 16)
            sp.dma_start(be_sb[:], be.unsqueeze(1).to_broadcast([P, 1])).then_inc(ld_c, 16)
            sp.dma_start(adj_in[:], adj[0:P, :]).then_inc(ld_adj, 16)
            sp.dma_start(x_row[:], x[0:P, :]).then_inc(ld_x0, 16)
            sp.wait_ge(dve_c, 1)
            sp.dma_start(kv_table[N:N + 1, :], zeros[0:1, :]).then_inc(st_c, 16)
            for i in range(TABLES):
                sp.dma_start(mask_table[i][N:N + 1, :], masked[:]).then_inc(st_c, 16)
            xg = x.rearrange("(g j p) d -> g p j d", j=GT, p=P)
            qg = q_table.rearrange("(g j) s d (i a) q -> g s (d i) j (a q)", j=GT, a=HALVES)
            kvg = kv_table[0:N, :].rearrange("(t p) r -> t p r", p=P)
            def load_q(tile):
                for i in range(PARTS):
                    sp.dma_start(q_next[HD * i:HD * i + HD], q_table[tile].rearrange("s d h q -> d s h q")
                                 ).then_inc(ld_q, 16)

            for g in range(2):
                sp.dma_start(x_in[g][:], xg[g]).then_inc(ld_x[g], 16)

            def store_rows(g):
                for s in range(PARTS):
                    sp.wait_ge((q_hi, q_mid, q_low)[s], g * 2 + 2)
                    sp.dma_start(qg[g][s], q_out[s][:].rearrange("p j a q -> p j (a q)")).then_inc(st_q, 16)
                for j in range(GT):
                    sp.wait_ge(kv_low, g * GT + (j + 1))
                    sp.dma_start(kvg[g * GT + j], kv_out[j][:]).then_inc(st_kv[j], 16)

            def load_adj(f):
                sp.wait_ge(act_cast, f * 8)
                sp.dma_start(adj_in[:], adj[f * P:(f + 1) * P, :]).then_inc(ld_adj, 16)

            load_adj(1)
            with sp.Fori(0, G // 2 - 1) as gg:
                for odd in range(2):
                    sp.wait_ge(pe_xt, gg * 4 + (2 * odd + 2))
                    sp.dma_start(x_in[odd][:], xg[gg * 2 + (odd + 2)]).then_inc(ld_x[odd], 16)
                    store_rows(gg * 2 + odd)
            store_rows(G - 2)
            store_rows(G - 1)
            for f in range(2):
                sp.wait_ge(act_jt, f * 8 + 8)
                sp.dma_start(mask_rows_of(f), joined_t[:]).then_inc(st_mask, 16)
                load_adj(f + 2)
            sp.wait_ge(st_q, 16 * PARTS * G)
            load_q(0)

            def tile(t, place):
                last = T - TABLES + place if isinstance(t, int) else None
                if last is None or last + 1 < T:
                    sp.wait_ge(q_ready, t + 1)
                    load_q(t + 1)
                if last is None or last + 2 < T:
                    sp.wait_ge(act_jt, t * 8 + 24)
                    sp.dma_start(mask_rows_of((place + 2) % TABLES), joined_t[:]).then_inc(st_mask, 16)
                if last is None or last + 4 < T:
                    sp.wait_ge(act_cast, t * 8 + 32)
                    sp.dma_start(adj_in[:], adj[bass.ds(t * P + 4 * P, P), :]).then_inc(ld_adj, 16)
                if last is None or last + 1 < T:
                    sp.wait_ge(dve_ln, t * 8 + 9)
                    sp.dma_start(x_row[:], x[bass.ds(t * P + P, P), :]).then_inc(ld_x0, 16)
                sp.wait_ge(dve_ln, t * 8 + 16)
                sp.dma_start(out[bass.ds(t * P, P), :], y_out[:]).then_inc(st_out, 16)

            with sp.Fori(0, T // TABLES - 1) as four:
                for place in range(TABLES):
                    tile(four * TABLES + place, place)
            for place in range(TABLES):
                tile(T - TABLES + place, place)
            sp.wait_ge(st_out, 16 * (T + 1))
            sp.wait_ge(st_mask, 16 * T)
            sp.wait_ge(ld_q, QLOAD * T)

        @block.gpsimd
        def _(pool):
            pool.wait_ge(dve_c, 3)
            pool.affine_select(out=ident_f[:], in_=ident_f[:], compare_op=ALU.is_equal, fill=0.0, base=0,
                               pattern=[[-1, P]], channel_multiplier=1).then_inc(pool_c, 1)
            pool.affine_select(out=before[:], in_=before[:], compare_op=ALU.is_gt, fill=0.0, base=0,
                               pattern=[[1, P]], channel_multiplier=-1).then_inc(pool_c, 1)
            pool.iota(iota_chunk[:], [[1, NB]], base=0, channel_multiplier=0).then_inc(pool_c, 1)
            pool.iota(iota_slot[:], [[1, P]], base=0, channel_multiplier=0).then_inc(pool_c, 1)
            pool.iota(slot_id[:], [[P, NB]], base=0, channel_multiplier=1).then_inc(pool_c, 1)
            pool.iota(key_c[:], [[1, NB]], base=-N // 2, channel_multiplier=NB).then_inc(pool_c, 1)
            pool.wait_ge(st_c, 16 + 16 * TABLES)
            for j in range(GT):
                pool.wait_ge(st_kv[j], 16 * G)

            def item(b, first, r, it):
                n8, t = pool.snap(r["n8"]), pool.snap(r["t"])
                if first:
                    pool.reg_mov(r["off"], (t & (TABLES - 1)) * NB)
                else:
                    pool.reg_add(r["off"], r["off"], CHUNKS)
                off = pool.snap(r["off"])
                wait_alone(pool, (pe_pv, n8 + (A_PV - 16)))
                pool.tensor_copy(picks[b][:], lists[:, bass.ds(off, CHUNKS)]).then_inc(picked, 8)
                wait_alone(pool, (picked, n8 + 8))
                for c in range(CHUNKS):
                    pool.indirect_dma_start(kv[b][:, c, :], None, kv_table,
                                            bass.IndirectOffsetOnAxis(ap=picks[b][:, c:c + 1], axis=0)
                                            ).then_inc(landed[b], 16)
                def mask_gather(i):
                    for c in range(CHUNKS):
                        pool.indirect_dma_start(mrow[b][:, c, :], None, mask_table[i],
                                                bass.IndirectOffsetOnAxis(ap=picks[b][:, c:c + 1], axis=0)
                                                ).then_inc(landed[b], 16)
                for upper in range(2):
                    middle = pool.snap(r["off"]) < 2 * NB if upper == 0 else pool.snap(r["off"]) >= 2 * NB
                    with pool.If(middle):
                        for i in (2 * upper, 2 * upper + 1):
                            edge = (2 * upper + 1) * NB
                            with pool.If(pool.snap(r["off"]) < edge if i % 2 == 0 else pool.snap(r["off"]) >= edge):
                                mask_gather(i)
                with in_last_item(pool, r):
                    pool.sem_inc(lists_read, 1)
                    end_of_tile(pool, r)

            def inner(r):
                with pool.If(pool.snap(r["t"]) < T):
                    load_count(pool)(r)
                    wait_alone(pool, (st_mask, pool.snap(r["t"]) * 16 + 16))
                with pool.If(pool.snap(r["t"]) >= T):
                    pool.reg_mov(r["nm"], 1)
            pool.sem_inc(lists_read, TABLES - 1)
            run_items(pool, item, inner, tiles=T + 1)

        @block.scalar
        def _(act):
            act.wait_ge(dve_c, 1)
            act.activation(std[:], eps[:], ACT.Sqrt)
            act.wait_ge(ld_adj, 16)
            act.activation(joined[:], adj_in[:], ACT.Sign, bias=minus_half[:]).then_inc(act_cast, 8)
            def x_copy(g, odd, c):
                act.wait_ge(pe_xt, g * 2 + (c + 1))
                act.copy(x_t[odd][:, c, :], ps_k[:]).then_inc(xt_copied, 1)

            def group(g, odd, more):
                if more:
                    x_copy(g + 1, 1 - odd, 0)
                act.wait_ge(st_q, g * (16 * PARTS))
                for a in range(HALVES):
                    act.wait_ge(pe_q, g * 8 + (4 * a + 4))
                    act.copy(q_out[0][:, :, a, :], ps_o[a][:].rearrange("p (j q) -> p j q", j=GT)
                             ).then_inc(q_hi, 1)
                if more:
                    x_copy(g + 1, 1 - odd, 1)
                for a in range(HALVES):
                    act.wait_ge(q_rested, g * 2 + (a + 1))
                    act.copy(q_out[1][:, :, a, :], q_rest[a][:].rearrange("p (j q) -> p j q", j=GT)
                             ).then_inc(q_mid, 1)

                def value(j):
                    act.wait_ge(pe_v, g * GT + (j + 1))
                    act.wait_ge(kv_rested, g * GT + max(j - 1, 0))
                    act.copy(kv_f[j % 2][:, D:2 * D], ps_t[j % 2][:, 0:D]).then_inc(v_copied, 1)

                def high(j):
                    act.wait_ge(v_copied, g * GT + (j + 1))
                    act.wait_ge(k_done, g * GT + (j + 1))
                    act.wait_ge(st_kv[j], g * 16)
                    act.copy(head_rows(kv_out[j], HIGH), heads(kv_f[j % 2])).then_inc(kv_hi, 1)

                def middle(j):
                    act.wait_ge(kv_rested, g * GT + (j + 1))
                    act.copy(head_rows(kv_out[j], MID), heads(kv_rest[j % 2])).then_inc(kv_mid, 1)

                value(0)
                for j in range(GT + 1):
                    if j + 1 < GT:
                        value(j + 1)
                    if j < GT:
                        high(j)
                    if j > 0:
                        middle(j - 1)

            for c in range(HALVES):
                x_copy(0, 0, c)
            with act.Fori(0, G // 2 - 1) as gg:
                for odd in range(2):
                    group(gg * 2 + odd, odd, True)
            group(G - 2, 0, True)
            group(G - 1, 1, False)

            def fe_cast(f8, f16):
                act.wait_ge(ld_adj, f16 + 16)
                act.wait_ge(pe_cnt, f8)
                act.activation(joined[:], adj_in[:], ACT.Sign, bias=minus_half[:]).then_inc(act_cast, 8)

            def joined_group(f8, g):
                act.wait_ge(pe_jt, f8 + 2 * g + 2)
                act.activation(joined_t[:, 8 * g:8 * g + 8, :].rearrange("p b q -> p (b q)"), as_bf16(ps_fe),
                               ACT.Copy, bias=-0.5, scale=0.5).then_inc(act_jt, 2)

            def row_std(l8):
                act.wait_ge(dve_ln, l8 + 3)
                act.activation(std[:], mean_var[:, 1:2], ACT.Sqrt, bias=eps[:]).then_inc(act_std, 8)

            def k_pair(next8, nb, p):
                act.wait_ge(pe_kt, next8 + (2 * p + 2))
                act.copy(k_t[nb][:, 2 * p:2 * p + 2, :].rearrange("p h k -> p (h k)"), as_bf16(ps_k)[0:HP, :]
                         ).then_inc(act_kt, 2)

            def mask_of(next8, nb):
                act.wait_ge(pe_mask, next8 + 8)
                act.activation(mask[nb][:], ps_k[:], ACT.Identity, bias=be_sb[:]).then_inc(act_mask, 8)

            act.wait_ge(ld_c, 32)
            for f in range(2):
                if f > 0:
                    act.wait_ge(st_mask, 16 * f)
                for g in range(4):
                    joined_group(8 * f, g)
                fe_cast(8 * f + 8, 16 * f + 16)
            mask_of(0, 0)
            for p in range(PAIRS):
                k_pair(0, 0, p)

            def item(b, first, r, it):
                n8, t = act.snap(r["n8"]), act.snap(r["t"])
                next8 = n8 + 8
                nb = (b + 1) % RING
                f8 = t * 8 + 16

                def next_cast():
                    with act.If(act.snap(r["t"]) < T - 3):
                        fe_cast(t * 8 + 24, t * 16 + 48)

                def pair(p):
                    act.wait_ge(pe_hard_t, n8 + (2 * p + 2 + A_HT))
                    act.wait_ge(pe_pv, n8 + (2 * p - 2 + A_PV))
                    act.copy(hard_t[p % 2][:], as_bf16(ps_t[p % 2])).then_inc(act_hard_t, 2)

                def next_k(p):
                    if first:
                        with act.If(act.snap(r["nm"]) > 1):
                            k_pair(next8, nb, p)
                    else:
                        k_pair(next8, nb, p)

                if first:
                    with act.If(act.snap(r["nm"]) > 1):
                        mask_of(next8, nb)
                    def group(g):
                        with act.If(t < T - 2):
                            if g == 0:
                                act.wait_ge(st_mask, t * 16 + 32)
                            joined_group(f8, g)

                    pair(0)
                    next_k(0)
                    group(0)
                    pair(1)
                    next_k(1)
                    group(1)
                    row_std(t * 8)
                    pair(2)
                    next_k(2)
                    group(2)
                    next_k(3)
                    group(3)
                    pair(3)
                    with act.If(act.snap(r["nm"]) < 2):
                        mask_of(next8, nb)
                        for p in range(PAIRS):
                            k_pair(next8, nb, p)
                        next_cast()
                        end_of_tile(act, r)
                else:
                    mask_of(next8, nb)
                    for p in range(PAIRS - 1):
                        pair(p)
                        next_k(p)
                    next_k(3)
                    pair(3)
                    with in_last_item(act, r):
                        next_cast()
                        end_of_tile(act, r)

            run_items(act, item, load_count(act), closing=lambda b, n8: row_std(8 * T))

        @block.vector
        def _(dve):
            dve.memset(zeros[:], 0.0)
            dve.memset(minus_half[:], -0.5)
            dve.memset(eps[:], EPS)
            dve.memset(mean_var[:], 0.0)
            dve.memset(hard_t[1][:], 0.0)
            dve.memset(kv[RING - 1][:, :, KW + 6 * HP:], 0.0)
            dve.memset(o_run[:], 0.0)
            dve.memset(keep[:], 0.0)
            dve.memset(ones_nb[:], 1.0)
            dve.memset(ones_b[:], 1.0)
            dve.memset(masked[:], -1.0).then_inc(dve_c, 1)
            dve.memset(ones_f[:], 1.0)
            dve.memset(before[:], 1.0).then_inc(dve_c, 1)
            dve.memset(ident_f[:], 1.0).then_inc(dve_c, 1)
            dve.wait_ge(pool_c, 6)
            dve.tensor_copy(iota_chunk_h[:], iota_chunk[:])
            dve.tensor_copy(iota_slot_h[:], iota_slot[:])
            dve.tensor_copy(key_h[:], key_c[:])
            dve.tensor_copy(ident_b[:], ident_f[:]).then_inc(dve_c, 1)
            dve.tensor_scalar(ident_big[:], ident_f[:], BIG, None, ALU.mult).then_inc(dve_c, 1)
            for i in range(3):
                dve.wait_ge(pe_w, i + 1)
                if i == 0:
                    for c in range(HALVES):
                        done = dve.tensor_copy(
                            w_t[0][:, c, :].rearrange("p (a d i) -> p a d i", a=HALVES, d=HD),
                            ps_s[0][:, c * D:c * D + D].rearrange("p (i a d) -> p a d i", a=HALVES, d=HD))
                    done.then_inc(dve_w, 1)
                else:
                    dve.tensor_copy(w_t[i][:].rearrange("p a e -> p (a e)"), (ps_s + ps_t)[i][:]).then_inc(dve_w, 1)
            dve.wait_ge(ld_c, 32)
            with dve.Fori(0, G) as g:
                for a in range(HALVES):
                    dve.wait_ge(q_hi, g * 2 + (a + 1))
                    dve.tensor_tensor(q_rest[a][:].rearrange("p (j q) -> p j q", j=GT),
                                      ps_o[a][:].rearrange("p (j q) -> p j q", j=GT), q_out[0][:, :, a, :],
                                      ALU.subtract).then_inc(q_rested, 1)
                for a in range(HALVES):
                    dve.wait_ge(q_mid, g * 2 + (a + 1))
                    dve.tensor_tensor(q_out[2][:, :, a, :], q_rest[a][:].rearrange("p (j q) -> p j q", j=GT),
                                      q_out[1][:, :, a, :], ALU.subtract).then_inc(q_low, 1)

                def k_row(j):
                    dve.wait_ge(pe_k, g * GT + (j + 1))
                    dve.wait_ge(kv_rested, g * GT + max(j - 1, 0))
                    dve.scalar_tensor_tensor(out=kv_f[j % 2][:, 0:D], in0=ps_s[j % 2][:, 0:D], scalar=SCALE,
                                             in1=we_sb[:], op0=ALU.mult, op1=ALU.add).then_inc(k_done, 1)

                def rest(j):
                    dve.wait_ge(kv_hi, g * GT + (j + 1))
                    dve.wait_ge(kv_low, g * GT + max(j - 1, 0))
                    dve.tensor_tensor(heads(kv_rest[j % 2]), heads(kv_f[j % 2]), head_rows(kv_out[j], HIGH),
                                      ALU.subtract).then_inc(kv_rested, 1)

                def low(j):
                    dve.wait_ge(kv_mid, g * GT + (j + 1))
                    dve.tensor_tensor(head_rows(kv_out[j], LOW), heads(kv_rest[j % 2]),
                                      head_rows(kv_out[j], MID), ALU.subtract).then_inc(kv_low, 1)

                k_row(0)
                for j in range(GT + 1):
                    if j + 1 < GT:
                        k_row(j + 1)
                    if j < GT:
                        rest(j)
                    if j > 0:
                        low(j - 1)

            def fe_scan(f8, f16):
                dve.wait_ge(pe_cnt, f8 + 8)
                dve.tensor_scalar(flag[:], ps_fe[:, 0:NB], 1.0 - P, None, ALU.is_gt).then_inc(dve_fe, 1)
                dve.wait_ge(dve_fe, f16 + 1)
                dve.tensor_tensor_scan(prefix[:], ones_nb[:], flag[:], 0.0, ALU.mult, ALU.add).then_inc(dve_fe, 1)

            def fe_hot(f8, f16, f):
                dve.wait_ge(pe_base, f8 + 8)
                dve.scalar_tensor_tensor(out=rank1[:], in0=prefix[:], scalar=ps_fe[:, 64:65], in1=flag[:],
                                         op0=ALU.add, op1=ALU.mult).then_inc(dve_fe, 1)
                dve.wait_ge(dve_fe, f16 + 3)
                dve.tensor_scalar(rank[:], rank1[:], -1.0, None, ALU.add).then_inc(dve_fe, 1)
                dve.wait_ge(dve_fe, f16 + 4)
                dve.tensor_scalar(digits[:, 0], rank[:], 7, None, ALU.arith_shift_right)
                dve.tensor_scalar(digits[:, 1], rank[:], 127, None, ALU.bitwise_and).then_inc(dve_fe, 1)
                dve.wait_ge(dve_fe, f16 + 5)
                dve.tensor_copy(digits_h[:], digits[:]).then_inc(dve_fe, 1)
                dve.tensor_scalar(total_i[:], ps_fe[:, 65:66], float(SLOTS - 1), None, ALU.add).then_inc(dve_fe, 1)
                dve.wait_ge(dve_fe, f16 + 7)
                dve.tensor_tensor(hot_hi[:], digits_h[:, 0].unsqueeze(2).to_broadcast([P, NB, NB]),
                                  iota_chunk_h[:].unsqueeze(1).to_broadcast([P, NB, NB]),
                                  ALU.is_equal).then_inc(dve_fe, 1)
                dve.tensor_scalar(n_items[:, bass.ds(f, 1)], total_i[:], 9, None,
                                  ALU.arith_shift_right).then_inc(dve_fe, 1)
                dve.tensor_scalar(unused[:], slot_id[:], ps_fe[:, 65:66], float(N), ALU.is_ge,
                                  ALU.mult).then_inc(dve_fe, 1)
                dve.wait_ge(dve_fe, f16 + 8)
                dve.tensor_tensor(hot_key[:], hot_hi[:], key_h[:].unsqueeze(2).to_broadcast([P, NB, NB]),
                                  ALU.mult).then_inc(dve_fe, 1)
                dve.tensor_tensor(hot_lo[:], digits_h[:, 1].unsqueeze(2).to_broadcast([P, NB, P]),
                                  iota_slot_h[:].unsqueeze(1).to_broadcast([P, NB, P]),
                                  ALU.is_equal).then_inc(dve_fe, 1)

            def fe_list(f8, f16, f):
                dve.wait_ge(dve_fe, f16 + 12)
                dve.wait_ge(pe_list, f8 + 8)
                dve.scalar_tensor_tensor(out=list_f[:], in0=ps_fe[:, 128:128 + NB], scalar=float(N // 2),
                                         in1=unused[:], op0=ALU.add, op1=ALU.max).then_inc(dve_fe, 1)
                dve.wait_ge(dve_fe, f16 + 13)
                dve.wait_ge(lists_read, f)
                off = (f % TABLES if isinstance(f, int) else f & (TABLES - 1)) * NB
                dve.tensor_copy(lists[:, bass.ds(off, NB)], list_f[:]).then_inc(dve_fe, 3)

            fe_scan(0, 0)
            fe_hot(0, 0, 0)
            fe_list(0, 0, 0)
            fe_scan(8, 16)
            fe_hot(8, 16, 1)

            def merge(n8):
                for k in range(2):
                    dve.wait_ge(pe_pv, n8 + (4 * k + 4 - 8 + A_PV))
                    dve.tensor_reduce(o_item[:, 4 * k:4 * k + 4, :],
                                      ps_o[k][:, 0:4 * PARTS * HD].rearrange("p (h s d) -> p h d s", h=4, s=PARTS),
                                      AX.X, ALU.add).then_inc(dve_osum, 4)
                dve.wait_ge(dve_merge, n8)
                dve.wait_ge(dve_keep, n8)
                dve.tensor_tensor(o_run[:], o_run[:], keep[:].unsqueeze(2).to_broadcast([P, H, HD]),
                                  ALU.mult).then_inc(dve_merge, 4)
                dve.wait_ge(dve_osum, n8 + 8)
                dve.wait_ge(dve_merge, n8 + 4)
                dve.tensor_tensor(o_run[:], o_run[:], o_item[:], ALU.add).then_inc(dve_merge, 4)

            def norm_stats(l8, l16, n8):
                dve.wait_ge(ld_x0, l16)
                dve.wait_ge(dve_merge, n8 + 8)
                dve.scalar_tensor_tensor(out=y[:], in0=o_run[:].rearrange("p h d -> p (h d)"), scalar=1.0 / H,
                                         in1=x_row[:], op0=ALU.mult, op1=ALU.add).then_inc(dve_ln, 1)
                dve.wait_ge(dve_ln, l8 + 1)
                dve.bn_stats(stats[:], y[:]).then_inc(dve_ln, 1)
                wait_alone(dve, (dve_ln, l8 + 2)) if not isinstance(l8, int) else dve.wait_ge(dve_ln, l8 + 2)
                dve.bn_aggr(mean_var[:], stats[:]).then_inc(dve_ln, 1)

            def norm_apply(l8, l16):
                dve.wait_ge(act_std, l8 + 8)
                dve.reciprocal(rstd[:], std[:]).then_inc(dve_ln, 1)
                dve.wait_ge(dve_ln, l8 + 4)
                dve.wait_ge(st_out, l16)
                dve.tensor_scalar(y_out[:], y[:], mean_var[:, 0:1], rstd[:, 0:1], ALU.subtract,
                                  ALU.mult).then_inc(dve_ln, 4)

            def take_q(landed_tiles, scores_done):
                dve.wait_ge(ld_q, landed_tiles)
                dve.wait_ge(pe_score, scores_done)
                dve.tensor_copy(q_cur[:].rearrange("p s h q -> p (s h q)"),
                                q_next[:].rearrange("p s h q -> p (s h q)")).then_inc(q_ready, 1)

            take_q(QLOAD, 0)
            dve.sem_inc(dve_top, A_TOP)
            dve.sem_inc(dve_ln, 8)
            dve.sem_inc(st_out, 16)

            def item(b, first, r, it):
                n8, t = dve.snap(r["n8"]), dve.snap(r["t"])
                nb = (b + 1) % RING
                f8, f16 = t * 8 + 16, t * 16 + 32

                def tops(p):
                    for h in (2 * p, 2 * p + 1):
                        wait_alone(dve, (pe_score, n8 + (h + 1)), *[(act_mask, n8 + 8)][:h == 0])
                        dve.tensor_tensor_reduce(out=score[h % 4][:], in0=ps_s[h % 2][:], in1=mask[b][:], scale=1.0,
                                                 scalar=FLOOR if first else top[b - 1][:, h:h + 1], op0=ALU.add, op1=ALU.max,
                                                 accum_out=top[b][:, h:h + 1]).then_inc(dve_top, 1)

                def hards(p):
                    dve.wait_ge(pe_hard_t, n8 + (2 * p - 2 + A_HT))
                    for h in (2 * p, 2 * p + 1):
                        dve.wait_ge(dve_top, n8 + (h + 1 + A_TOP))
                        if h == H - 1:
                            if first:
                                dve.memset(keep[:], 0.0).then_inc(dve_keep, 8)
                            else:
                                dve.tensor_tensor(keep[:], top[b - 1][:], top[b][:], ALU.is_equal
                                                  ).then_inc(dve_keep, 8)
                        dve.tensor_scalar(hard[h % 4][:], score[h % 4][:], top[b][:, h:h + 1], None,
                                          ALU.is_equal).then_inc(dve_hard, 1)

                for p in range(PAIRS):
                    tops(p)
                    hards(p)
                    if p == 0 and first:
                        with dve.If(t < T - 1):
                            fe_list(t * 8 + 8, t * 16 + 16, t + 1)
                    if p == 1:
                        merge(n8)
                        if first:
                            with dve.If(t > 0):
                                norm_stats(t * 8, t * 16, n8)
                if first:
                    with dve.If(t > 0):
                        norm_apply(t * 8, t * 16)

                def last_item():
                    with dve.If(t < T - 2):
                        fe_scan(f8, f16)
                    with dve.If(t < T - 1):
                        take_q(t * QLOAD + 2 * QLOAD, n8 + 8)
                    with dve.If(t < T - 2):
                        fe_hot(f8, f16, t + 2)
                    end_of_tile(dve, r)

                if first:
                    with dve.If(dve.snap(r["nm"]) < 2):
                        last_item()
                else:
                    with in_last_item(dve, r):
                        last_item()

            def closing(b, n8):
                merge(n8)
                norm_stats(8 * T, 16 * T, n8)
                norm_apply(8 * T, 16 * T)
            run_items(dve, item, load_count(dve), closing=closing)

        @block.tensor
        def _(pe):
            pe.wait_ge(pool_c, 6)
            pe.wait_ge(dve_c, 5)
            for k in range(2):
                mm = pe.matmul(ps_o[k][:, 0:384], ident_b[:], zeros[:, 0:384], start=True, stop=True)
            mm.then_inc(pe_pv, A_PV - 2)
            pe.wait_ge(ld_w, 48)
            for i in range(3):
                for a in range(HALVES):
                    for c in range(HALVES):
                        mm = pe.transpose((ps_s + ps_t)[i][:, c * D + a * P:c * D + a * P + P],
                                          w_sb[i][:, a, c * P:c * P + P], ident_f[:])
                mm.then_inc(pe_w, 1)
            pe.wait_ge(dve_w, 3)
            pe.wait_ge(pe_pv, A_PV - 2)
            def x_half(g, uses, odd, c):
                if c == 0:
                    pe.wait_ge(ld_x[odd], uses)
                pe.wait_ge(xt_copied, g * 2 + c)
                for j in range(GT):
                    mm = pe.transpose(ps_k[:, j * P:j * P + P], x_in[odd][:, j, c * P:c * P + P], ident_f[:])
                mm.then_inc(pe_xt, 1)

            def group(g, gg, odd, more):
                if more:
                    x_half(g + 1, (gg + odd) * 16 + 16, 1 - odd, 0)
                pe.wait_ge(xt_copied, g * 2 + 2)
                pe.wait_ge(q_rested, g * 2)
                for a in range(HALVES):
                    for c in range(HALVES):
                        mm = pe.matmul(ps_o[a][:], w_t[0][:, c, a * P:a * P + P], x_t[odd][:, c, :],
                                       start=(c == 0), stop=(c == 1))
                    mm.then_inc(pe_q, 4)
                if more:
                    x_half(g + 1, (gg + odd) * 16 + 16, 1 - odd, 1)
                for j in range(GT):
                    pe.wait_ge(k_done, g * GT + max(j - 1, 0))
                    pe.wait_ge(v_copied, g * GT + max(j - 1, 0))
                    for i, bank, done in ((1, ps_s, pe_k), (2, ps_t, pe_v)):
                        for c in range(HALVES):
                            mm = pe.matmul(bank[j % 2][:, 0:D], x_t[odd][:, c, j * P:j * P + P], w_t[i][:, c, :],
                                           start=(c == 0), stop=(c == 1))
                        mm.then_inc(done, 1)

            for c in range(HALVES):
                x_half(0, 16, 0, c)
            with pe.Fori(0, G // 2 - 1) as gg:
                for odd in range(2):
                    group(gg * 2 + odd, gg, odd, True)
            group(G - 2, G // 2 - 1, 0, True)
            group(G - 1, G // 2 - 1, 1, False)

            blocks = joined[:].rearrange("q (p b) -> q b p", b=NB)

            def fe_transpose(f8, f16, g):
                if g == 0:
                    pe.wait_ge(act_cast, f8 + 8)
                    pe.wait_ge(dve_fe, f16)
                else:
                    pe.wait_ge(act_jt, f8 + 2 * g)
                for b in range(8):
                    mm = pe.transpose(as_bf16(ps_fe)[:, b * P:b * P + P], blocks[:, 8 * g + b, :], ident_b[:])
                mm.then_inc(pe_jt, 2)

            def fe_count(f8):
                pe.wait_ge(act_jt, f8 + 8)
                for b in range(NB):
                    mm = pe.matmul(ps_fe[:, b:b + 1], blocks[:, b, :], ones_b[:], start=True, stop=True)
                mm.then_inc(pe_cnt, 8)

            def fe_base(f8, f16):
                pe.wait_ge(dve_fe, f16 + 2)
                pe.matmul(ps_fe[:, 64:65], before[:], prefix[:, NB - 1:NB], start=True, stop=True)
                pe.matmul(ps_fe[:, 65:66], ones_f[:], prefix[:, NB - 1:NB], start=True,
                          stop=True).then_inc(pe_base, 8)

            def fe_list(f8, f16):
                pe.wait_ge(dve_fe, f16 + 12)
                for b in range(NB):
                    mm = pe.matmul(ps_fe[:, 128:128 + NB], hot_lo[:, b, :], hot_key[:, b, :], start=(b == 0),
                                   stop=(b == NB - 1))
                mm.then_inc(pe_list, 8)

            def k_pair(n8, nb, p):
                if p == 0:
                    pe.wait_ge(act_mask, n8 + 8)
                else:
                    pe.wait_ge(act_kt, n8 + 2 * p)
                for h in (2 * p, 2 * p + 1):
                    for c in range(CHUNKS):
                        at = (h % 2) * SLOTS + c * P
                        mm = pe.transpose(as_bf16(ps_k)[0:HP, at:at + P],
                                          kv[nb][:, c, h * HP:(h + 1) * HP], ident_b[:])
                mm.then_inc(pe_kt, 2)

            def mask_rows(n8, nb, uses):
                pe.wait_ge(landed[nb], uses)
                pe.wait_ge(act_kt, n8)
                for c in range(CHUNKS):
                    mm = pe.matmul(ps_k[:, c * P:c * P + P], mrow[nb][:, c, :], ident_big[:], start=True, stop=True)
                mm.then_inc(pe_mask, 8)

            def scores(n8, b, h):
                pe.wait_ge(dve_top, n8 + (h - 1 + A_TOP))
                if h % 2 == 0:
                    pe.wait_ge(act_kt, n8 + (h + 2))
                for i in range(PARTS):
                    mm = pe.matmul(ps_s[h % 2][:], q_cur[:, i, h, :], k_t[b][:, h, :], start=(i == 0),
                                   stop=(i == PARTS - 1))
                mm.then_inc(pe_score, 1)

            def values(n8, b, p):
                at8 = n8 + 8
                pe.wait_ge(act_hard_t, at8 + (2 * p + 2 + A_HC - 8))
                if p % 2 == 0:
                    pe.wait_ge(dve_osum, at8 + (2 * p + 4 - 8))
                for h in (2 * p, 2 * p + 1):
                    for c in range(CHUNKS):
                        at = (h % 2) * SLOTS + c * P
                        mm = pe.matmul(ps_o[h // 4][:, (h % 4) * HP:(h % 4 + 1) * HP],
                                       hard_t[p % 2][:, at:at + P],
                                       kv[b][:, c, KW + h * HP:KW + (h + 1) * HP],
                                       start=(c == 0), stop=(c == CHUNKS - 1))
                mm.then_inc(pe_pv, 2)

            for f in range(2):
                for g in range(4):
                    fe_transpose(8 * f, 16 * f, g)
                fe_count(8 * f)
                fe_base(8 * f, 16 * f)
                if f == 0:
                    fe_list(0, 0)
            mask_rows(0, 0, 128)
            for p in range(PAIRS):
                k_pair(0, 0, p)
            pe.sem_inc(pe_hard_t, A_HT)
            pe.sem_inc(act_hard_t, A_HC)
            pe.wait_ge(q_ready, 1)
            scores(0, 0, 0)
            scores(0, 0, 1)

            def item(b, first, r, it):
                n8, t = pe.snap(r["n8"]), pe.snap(r["t"])
                next8 = n8 + 8
                nb = (b + 1) % RING
                uses = it * 128 + (128 if b < RING - 1 else 256)
                f8, f16 = t * 8 + 16, t * 16 + 32

                def transposes(p):
                    pe.wait_ge(dve_hard, n8 + (2 * p + 2))
                    pe.wait_ge(act_hard_t, n8 + (2 * p - 2 + A_HC))
                    for h in (2 * p, 2 * p + 1):
                        for c in range(CHUNKS):
                            at = (h % 2) * SLOTS + c * P
                            mm = pe.transpose(as_bf16(ps_t[p % 2])[:, at:at + P], hard[h % 4][:, c * P:c * P + P],
                                              ident_b[:])
                    mm.then_inc(pe_hard_t, 2)

                def next_tile_q():
                    with pe.If(pe.snap(r["t"]) < T):
                        pe.wait_ge(q_ready, pe.snap(r["t"]) + 1)

                def next_k(p):
                    if first:
                        with pe.If(pe.snap(r["nm"]) > 1):
                            k_pair(next8, nb, p)
                    else:
                        k_pair(next8, nb, p)

                def front_end(before, stage):
                    if first:
                        with pe.If(t < before):
                            stage()

                front_end(T - 1, lambda: fe_list(t * 8 + 8, t * 16 + 16))
                scores(n8, b, 2)
                scores(n8, b, 3)
                values(n8 - 8, (b - 1) % RING, 3)
                if first:
                    with pe.If(pe.snap(r["nm"]) > 1):
                        mask_rows(next8, nb, uses)
                else:
                    mask_rows(next8, nb, uses)
                transposes(0)
                next_k(0)
                front_end(T - 2, lambda: fe_transpose(f8, f16, 0))
                scores(n8, b, 4)
                scores(n8, b, 5)
                transposes(1)
                next_k(1)
                front_end(T - 2, lambda: fe_transpose(f8, f16, 1))
                values(n8, b, 0)
                scores(n8, b, 6)
                scores(n8, b, 7)
                transposes(2)
                next_k(2)
                if first:
                    with pe.If(pe.snap(r["nm"]) > 1):
                        scores(next8, nb, 0)
                        scores(next8, nb, 1)
                    front_end(T - 2, lambda: fe_transpose(f8, f16, 2))
                else:
                    with in_last_item(pe, r):
                        with pe.If(t < T - 2):
                            fe_count(f8)
                            fe_base(f8, f16)
                        end_of_tile(pe, r)
                        next_tile_q()
                    scores(next8, nb, 0)
                    scores(next8, nb, 1)
                values(n8, b, 1)
                next_k(3)
                front_end(T - 2, lambda: fe_transpose(f8, f16, 3))
                transposes(3)
                values(n8, b, 2)
                if first:
                    with pe.If(pe.snap(r["nm"]) < 2):
                        with pe.If(t < T - 2):
                            fe_count(f8)
                            fe_base(f8, f16)
                        mask_rows(next8, nb, uses)
                        for p in range(PAIRS):
                            k_pair(next8, nb, p)
                        end_of_tile(pe, r)
                        next_tile_q()
                        scores(next8, nb, 0)
                        scores(next8, nb, 1)

            run_items(pe, item, load_count(pe), closing=lambda b, n8: values(n8 - 8, (b - 1) % RING, 3))


_INS = ["x", "adj", "L0_gnn_WQ", "L0_gnn_WK", "L0_gnn_WV", "L0_gnn_we", "L0_gnn_be"]


def kernel(**inputs):
    import numpy as np
    import concourse.bacc as bacc
    from concourse.bass_utils import run_bass_kernel_spmd

    nc = bacc.Bacc("TRN2", target_bir_lowering=False, num_devices=1)
    arrays, args = {}, []
    for name in _INS:
        a = np.ascontiguousarray(inputs[name])
        arrays[f"in_{name}"] = a
        args.append(nc.dram_tensor(f"in_{name}", a.shape, mybir.dt.from_np(a.dtype), kind="ExternalInput").ap())
    args.append(nc.dram_tensor("out_0", inputs["x"].shape, mybir.dt.float32, kind="ExternalOutput").ap())
    hard_attention(nc, *args)
    r = run_bass_kernel_spmd(nc, [arrays], core_ids=[0])
    return r.results[0]["out_0"]
```

```python
from contextlib import ExitStack

import concourse.bass as bass
from concourse import mybir

ALU = mybir.AluOpType
ACT = mybir.ActivationFunctionType
AX = mybir.AxisListType
F32 = mybir.dt.float32
BF16 = mybir.dt.bfloat16
F16 = mybir.dt.float16
I32 = mybir.dt.int32
U32 = mybir.dt.uint32

P = 128
HD = 32
STACKS = 2
PARTS = 3
CHUNKS = 4
SLOTS = CHUNKS * P
RING = 3
TABLES = 4
EPS = 1e-5
BIG = 2.0 ** 100
FLOOR = -(2.0 ** 90)


def hard_attention(nc, x, adj, wq, wk, wv, we, be, out):
    N, D = x.shape
    H = D // HD
    T = N // P
    NB = N // P
    HALVES = D // P
    PAIRS = H // 2
    HP = PARTS * HD
    HR = P + HP
    WIDE = 2 * P + NB - 1
    ROW = H * HR
    TURNS_INNER = 8
    TURNS_OUTER = -(-(T * (N // SLOTS) + 2) // (RING * TURNS_INNER))
    GT = 4
    G = T // GT
    SCALE = float(HD) ** -0.5
    assert D == 256 and N == 4096 and SLOTS == 512 and H == 8

    kv_table = nc.dram_tensor("kv_table", (N + 1, ROW), BF16, kind="Internal").ap()
    mask_table = [nc.dram_tensor(f"mask_table{i}", (N + 1, P), BF16, kind="Internal").ap() for i in range(TABLES)]
    q_table = nc.dram_tensor("q_table", (T, PARTS, HD, H, P), BF16, kind="Internal").ap()

    with ExitStack() as ctx:
        def sb(name, shape, dt):
            return ctx.enter_context(nc.sbuf_tensor(name, shape, dt))

        def pb(name, dt=F32):
            return ctx.enter_context(nc.psum_tensor(name, [P, 512], dt))

        def sem(name):
            return ctx.enter_context(nc.semaphore(name))

        ident_f = sb("ident_f", [P, P], F32)
        ident_b = sb("ident_b", [P, P], BF16)
        ident_big = sb("ident_big", [P, P], BF16)
        before = sb("before", [P, P], F32)
        ones_f = sb("ones_f", [P, P], F32)
        ones_b = sb("ones_b", [P, 1], BF16)
        iota = sb("iota", [P, WIDE], I32)
        slot_id = sb("slot_id", [P, NB], I32)
        first_key = sb("first_key", [P, 1], I32)
        iota_h = sb("iota_h", [P, WIDE], F16)
        iota_1 = sb("iota_1", [P, NB], F32)
        first_key_f = sb("first_key_f", [P, 1], F32)
        be_sb = sb("be_sb", [P, 1], F32)
        we_sb = sb("we_sb", [P, D], F32)
        zeros = sb("zeros", [P, ROW], BF16)
        minus_half = sb("minus_half", [P, 1], F32)
        eps = sb("eps", [P, 1], F32)
        masked = sb("masked", [1, P], BF16)
        w_sb = [sb(f"w{i}", [P, HALVES, D], F32) for i in range(3)]
        w_t = [sb(f"wt{i}", [P, HALVES, D], F32) for i in range(3)]
        x_in = [sb(f"x_in{i}", [P, GT, D], F32) for i in range(2)]
        x_t = [sb(f"x_t{i}", [P, HALVES, GT * P], F32) for i in range(2)]
        q_out = [sb(f"q_out{i}", [P, GT, HALVES, P], BF16) for i in range(PARTS)]
        kv_out = [sb(f"kv_out{i}", [P, ROW], BF16) for i in range(GT)]
        kv_f = [sb(f"kv_f{i}", [P, 2 * D], F32) for i in range(2)]
        adj_in = sb("adj_in", [P, N], I32)
        joined = sb("joined", [P, N], BF16)
        joined_t = sb("joined_t", [P, NB, P], BF16)
        flag = sb("flag", [P, NB], F32)
        listed = sb("listed", [P, 1], F32)
        found = [sb(f"found{i}", [P, NB], F32) for i in range(2)]
        order = sb("order", [P, NB], F32)
        real = sb("real", [P, NB], F32)
        keys = sb("keys", [P, NB], F16)
        rank0 = sb("rank0", [P, 1], I32)
        digits = sb("digits", [P, 2], I32)
        digits_f = sb("digits_f", [P, 2], F32)
        hot_lo = sb("hot_lo", [P, WIDE], F16)
        hot_hi = sb("hot_hi", [P, NB + 2], F16)
        hot_key = sb("hot_key", [P, NB, NB + 2], F16)
        total_i = sb("total_i", [P, 1], I32)
        n_items = sb("n_items", [P, T], I32)
        unused = sb("unused", [P, NB], F32)
        list_f = sb("list_f", [P, NB], F32)
        lists = sb("lists", [P, TABLES * NB], U32)
        picks = [sb(f"picks{i}", [P, CHUNKS], U32) for i in range(RING)]
        kv = [sb(f"kv{i}", [P, CHUNKS, ROW], BF16) for i in range(RING)]
        mrow = [sb(f"mrow{i}", [P, CHUNKS, P], BF16) for i in range(RING)]
        k_t = [sb(f"k_t{i}", [P, H, SLOTS], BF16) for i in range(RING)]
        mask = [sb(f"mask{i}", [P, SLOTS], F32) for i in range(RING)]
        q_next = sb("q_next", [P, STACKS, H, P], BF16)
        q_cur = sb("q_cur", [P, STACKS, H, P], BF16)
        score = [sb(f"score{i}", [P, SLOTS], F32) for i in range(4)]
        q_rest, kv_rest = score[0:2], score[2:4]
        hard = [sb(f"hard{i}", [P, SLOTS], BF16) for i in range(4)]
        hard_t = [sb(f"hard_t{i}", [P, 2 * SLOTS], BF16) for i in range(2)]
        top = [sb(f"top{i}", [P, H], F32) for i in range(RING)]
        keep = sb("keep", [P, H], F32)
        o_item = sb("o_item", [P, H, HD], F32)
        o_run = sb("o_run", [P, H, HD], F32)
        x_row = sb("x_row", [P, D], F32)
        y = sb("y", [P, D], F32)
        stats = sb("stats", [P, 6], F32)
        mean_var = sb("mean_var", [P, 2], F32)
        std = sb("std", [P, 1], F32)
        rstd = sb("rstd", [P, 1], F32)
        y_out = sb("y_out", [P, D], F32)

        ps_s = [pb("ps_s0"), pb("ps_s1")]
        ps_t = [pb("ps_t0"), pb("ps_t1")]
        ps_o = [pb("ps_o0"), pb("ps_o1")]
        ps_k = pb("ps_k")
        ps_fe = pb("ps_fe")

        def as_bf16(bank):
            return bank[:].bitcast(BF16)

        def heads(cols):
            return cols[:].rearrange("p (k h d) -> p h k d", k=2, d=HD)

        HIGH, MID, LOW = 0, 1, 2

        def part_of(row, part):
            return row[:].rearrange("p (h g d) -> p h g d", h=H, d=HD)[:, :, part:part + 5:4, :]

        def second_high(row):
            return row[:].rearrange("p (h g d) -> p h g d", h=H, d=HD)[:, :, 3, :]


        ld_w, ld_c, ld_x, ld_x0, ld_q = (
            sem("ld_w"), sem("ld_c"), [sem("ld_x_even"), sem("ld_x_odd")], sem("ld_x0"), sem("ld_q"))
        ld_adj = sem("ld_adj")
        pool_c, dve_c = sem("pool_c"), sem("dve_c")
        pe_w, dve_w = sem("pe_w"), sem("dve_w")
        pe_xt, xt_copied = sem("pe_xt"), sem("xt_copied")
        pe_q, st_q = sem("pe_q"), sem("st_q")
        q_hi, q_rested, q_mid, q_low = sem("q_hi"), sem("q_rested"), sem("q_mid"), sem("q_low")
        pe_k, pe_v, k_done, v_copied, kv_hi, kv_rested, kv_mid, kv_low = (
            sem("pe_k"), sem("pe_v"), sem("k_done"), sem("v_copied"), sem("kv_hi"), sem("kv_rested"),
            sem("kv_mid"), sem("kv_low"))
        st_kv = [sem(f"st_kv{j}") for j in range(GT)]
        st_c = sem("st_c")
        act_cast, pe_jt, act_jt, pe_cnt, dve_fe, pe_base, pe_list, st_mask, lists_read = (
            sem("act_cast"), sem("pe_jt"), sem("act_jt"), sem("pe_cnt"), sem("dve_fe"), sem("pe_base"),
            sem("pe_list"), sem("st_mask"), sem("lists_read"))
        picked = sem("picked")
        landed = [sem(f"landed{i}") for i in range(RING)]
        pe_kt, act_kt, pe_mask, act_mask = sem("pe_kt"), sem("act_kt"), sem("pe_mask"), sem("act_mask")
        pe_score, dve_top, dve_hard, pe_hard_t, act_hard_t, pe_pv = (
            sem("pe_score"), sem("dve_top"), sem("dve_hard"), sem("pe_hard_t"), sem("act_hard_t"), sem("pe_pv"))
        dve_osum, dve_merge, dve_keep, q_ready = sem("dve_osum"), sem("dve_merge"), sem("dve_keep"), sem("q_ready")
        dve_ln, act_std, st_out = sem("dve_ln"), sem("act_std"), sem("st_out")
        A_TOP, A_HT, A_HC, A_PV, A_MERGE, A_KEEP = 2, 4, 4, 17, 1, 1
        QLOAD = 16 * 4

        block = ctx.enter_context(nc.Block())

        scratch = {}

        def wait_alone(eng, *waits):
            name = str(eng.engine)
            if name not in scratch:
                scratch[name] = [eng.alloc_register(f"wait{i}") for i in range(2)]
            regs = scratch[name]
            for (_, value), reg in zip(waits, regs):
                eng.reg_mov(reg, value)
            eng.wait_ge(dve_c, 1)
            for (waited, _), reg in zip(waits, regs):
                eng.wait_ge(waited, reg)

        def run_items(eng, item, inner, tiles=T, closing=None):
            r = {k: eng.alloc_register(k) for k in ("n8", "left", "nm", "t", "off")}
            for k in r:
                eng.reg_mov(r[k], 0)
            end = tiles + (closing is not None)
            with eng.Fori(0, TURNS_OUTER) as outer:
                with eng.If(eng.snap(r["t"]) < end):
                    with eng.Fori(0, TURNS_INNER) as turn:
                        with eng.If(eng.snap(r["t"]) < end):
                            for b in range(RING):
                                place(eng, item, inner, tiles, closing, b, r, outer * TURNS_INNER + turn)

        def place(eng, item, inner, tiles, closing, b, r, it):
            with eng.If(eng.snap(r["left"]) > 0):
                item(b, False, r, it)
            with eng.If(eng.snap(r["left"]) < 1):
                if closing is not None:
                    with eng.If(eng.snap(r["t"]) >= tiles):
                        with eng.If(eng.snap(r["t"]) < tiles + 1):
                            closing(b, eng.snap(r["n8"]))
                            eng.reg_add(r["t"], r["t"], 1)
                with eng.If(eng.snap(r["t"]) < tiles):
                    inner(r)
                    eng.reg_mov(r["left"], r["nm"])
                    item(b, True, r, it)
            eng.reg_add(r["n8"], r["n8"], 8)
            eng.reg_add(r["left"], r["left"], -1)

        def end_of_tile(eng, r):
            eng.reg_add(r["t"], r["t"], 1)

        def in_last_item(eng, r):
            return eng.If(eng.snap(r["left"]) < 2)

        def load_count(eng):
            def load(r):
                wait_alone(eng, (dve_fe, eng.snap(r["t"]) * 16 + 16))
                eng.reg_load(r["nm"], n_items[0:1, bass.ds(eng.snap(r["t"]), 1)])
            return load

        def mask_rows_of(parity):
            return mask_table[parity][0:N, :].rearrange("(p b) q -> p b q", p=P)

        @block.sync
        def _(sp):
            for i, w in enumerate((wq, wk, wv)):
                sp.dma_start(w_sb[i][:], w.rearrange("(a p) d -> p a d", p=P)).then_inc(ld_w, 16)
            sp.dma_start(we_sb[:].rearrange("p (h d) -> p h d", h=H),
                         we.unsqueeze(1).to_broadcast([P, H, HD])).then_inc(ld_c, 16)
            sp.dma_start(be_sb[:], be.unsqueeze(1).to_broadcast([P, 1])).then_inc(ld_c, 16)
            sp.dma_start(adj_in[:], adj[0:P, :]).then_inc(ld_adj, 16)
            sp.dma_start(x_row[:], x[0:P, :]).then_inc(ld_x0, 16)
            sp.wait_ge(dve_c, 1)
            sp.dma_start(kv_table[N:N + 1, :], zeros[0:1, :]).then_inc(st_c, 16)
            for i in range(TABLES):
                sp.dma_start(mask_table[i][N:N + 1, :], masked[:]).then_inc(st_c, 16)
            xg = x.rearrange("(g j p) d -> g p j d", j=GT, p=P)
            qg = q_table.rearrange("(g j) s d (i a) q -> g s (d i) j (a q)", j=GT, a=HALVES)
            kvg = kv_table[0:N, :].rearrange("(t p) r -> t p r", p=P)
            def load_q(tile):
                parts = q_table[tile].rearrange("s d h q -> d s h q")
                for quarter, (stacks, own) in enumerate(((slice(0, 2), slice(HIGH, LOW + 1, 2)),
                                                         (slice(0, 2), slice(HIGH, LOW)),
                                                         (slice(0, 2), slice(HIGH, LOW)),
                                                         (slice(0, 1), slice(MID, LOW)))):
                    sp.dma_start(q_next[HD * quarter:HD * quarter + HD, stacks], parts[:, own]).then_inc(ld_q, 16)

            for g in range(2):
                sp.dma_start(x_in[g][:], xg[g]).then_inc(ld_x[g], 16)

            def store_rows(g):
                for s in range(PARTS):
                    sp.wait_ge((q_hi, q_mid, q_low)[s], g * 2 + 2)
                    sp.dma_start(qg[g][s], q_out[s][:].rearrange("p j a q -> p j (a q)")).then_inc(st_q, 16)
                for j in range(GT):
                    sp.wait_ge(kv_low, g * GT + (j + 1))
                    sp.dma_start(kvg[g * GT + j], kv_out[j][:]).then_inc(st_kv[j], 16)

            def load_adj(f):
                sp.wait_ge(act_cast, f * 8)
                sp.dma_start(adj_in[:], adj[f * P:(f + 1) * P, :]).then_inc(ld_adj, 16)

            load_adj(1)
            with sp.Fori(0, G // 2 - 1) as gg:
                for odd in range(2):
                    sp.wait_ge(pe_xt, gg * 4 + (2 * odd + 2))
                    sp.dma_start(x_in[odd][:], xg[gg * 2 + (odd + 2)]).then_inc(ld_x[odd], 16)
                    store_rows(gg * 2 + odd)
            store_rows(G - 2)
            store_rows(G - 1)
            for f in range(2):
                sp.wait_ge(act_jt, f * 8 + 8)
                sp.dma_start(mask_rows_of(f), joined_t[:]).then_inc(st_mask, 16)
                load_adj(f + 2)
            sp.wait_ge(st_q, 16 * PARTS * G)
            sp.wait_ge(dve_c, 1)
            load_q(0)

            def tile(t, place):
                last = T - TABLES + place if isinstance(t, int) else None
                if last is None or last + 1 < T:
                    sp.wait_ge(q_ready, t + 1)
                    load_q(t + 1)
                if last is None or last + 2 < T:
                    sp.wait_ge(act_jt, t * 8 + 24)
                    sp.dma_start(mask_rows_of((place + 2) % TABLES), joined_t[:]).then_inc(st_mask, 16)
                if last is None or last + 4 < T:
                    sp.wait_ge(act_cast, t * 8 + 32)
                    sp.dma_start(adj_in[:], adj[bass.ds(t * P + 4 * P, P), :]).then_inc(ld_adj, 16)
                if last is None or last + 1 < T:
                    sp.wait_ge(dve_ln, t * 8 + 9)
                    sp.dma_start(x_row[:], x[bass.ds(t * P + P, P), :]).then_inc(ld_x0, 16)
                sp.wait_ge(dve_ln, t * 8 + 16)
                sp.dma_start(out[bass.ds(t * P, P), :], y_out[:]).then_inc(st_out, 16)

            with sp.Fori(0, T // TABLES - 1) as four:
                for place in range(TABLES):
                    tile(four * TABLES + place, place)
            for place in range(TABLES):
                tile(T - TABLES + place, place)
            sp.wait_ge(st_out, 16 * (T + 1))
            sp.wait_ge(st_mask, 16 * T)
            sp.wait_ge(ld_q, QLOAD * T)

        @block.gpsimd
        def _(pool):
            pool.wait_ge(dve_c, 3)
            pool.affine_select(out=ident_f[:], in_=ident_f[:], compare_op=ALU.is_equal, fill=0.0, base=0,
                               pattern=[[-1, P]], channel_multiplier=1).then_inc(pool_c, 1)
            pool.affine_select(out=before[:], in_=before[:], compare_op=ALU.is_gt, fill=0.0, base=0,
                               pattern=[[1, P]], channel_multiplier=-1).then_inc(pool_c, 1)
            pool.iota(iota[:], [[1, WIDE]], base=0, channel_multiplier=0).then_inc(pool_c, 2)
            pool.iota(slot_id[:], [[P, NB]], base=0, channel_multiplier=1).then_inc(pool_c, 1)
            pool.iota(first_key[:], [[1, 1]], base=-N // 2 - 1, channel_multiplier=NB).then_inc(pool_c, 1)
            pool.wait_ge(st_c, 16 + 16 * TABLES)
            for j in range(GT):
                pool.wait_ge(st_kv[j], 16 * G)

            def item(b, first, r, it):
                n8, t = pool.snap(r["n8"]), pool.snap(r["t"])
                if first:
                    pool.reg_mov(r["off"], (t & (TABLES - 1)) * NB)
                else:
                    pool.reg_add(r["off"], r["off"], CHUNKS)
                off = pool.snap(r["off"])
                wait_alone(pool, (pe_pv, n8 + (A_PV - 16)))
                pool.tensor_copy(picks[b][:], lists[:, bass.ds(off, CHUNKS)]).then_inc(picked, 8)
                wait_alone(pool, (picked, n8 + 8))
                for c in range(CHUNKS):
                    pool.indirect_dma_start(kv[b][:, c, :], None, kv_table,
                                            bass.IndirectOffsetOnAxis(ap=picks[b][:, c:c + 1], axis=0)
                                            ).then_inc(landed[b], 16)
                def mask_gather(i):
                    for c in range(CHUNKS):
                        pool.indirect_dma_start(mrow[b][:, c, :], None, mask_table[i],
                                                bass.IndirectOffsetOnAxis(ap=picks[b][:, c:c + 1], axis=0)
                                                ).then_inc(landed[b], 16)
                for upper in range(2):
                    middle = pool.snap(r["off"]) < 2 * NB if upper == 0 else pool.snap(r["off"]) >= 2 * NB
                    with pool.If(middle):
                        for i in (2 * upper, 2 * upper + 1):
                            edge = (2 * upper + 1) * NB
                            with pool.If(pool.snap(r["off"]) < edge if i % 2 == 0 else pool.snap(r["off"]) >= edge):
                                mask_gather(i)
                with in_last_item(pool, r):
                    pool.sem_inc(lists_read, 1)
                    end_of_tile(pool, r)

            def inner(r):
                with pool.If(pool.snap(r["t"]) < T):
                    load_count(pool)(r)
                    wait_alone(pool, (st_mask, pool.snap(r["t"]) * 16 + 16))
                with pool.If(pool.snap(r["t"]) >= T):
                    pool.reg_mov(r["nm"], 1)
            pool.sem_inc(lists_read, TABLES - 1)
            run_items(pool, item, inner, tiles=T + 1)

        @block.scalar
        def _(act):
            act.wait_ge(dve_c, 1)
            act.activation(std[:], eps[:], ACT.Sqrt)
            act.wait_ge(ld_adj, 16)
            act.activation(joined[:], adj_in[:], ACT.Sign, bias=minus_half[:]).then_inc(act_cast, 8)
            def x_copy(g, odd, c):
                act.wait_ge(pe_xt, g * 2 + (c + 1))
                act.copy(x_t[odd][:, c, :], ps_k[:]).then_inc(xt_copied, 1)

            def group(g, odd, more):
                if more:
                    x_copy(g + 1, 1 - odd, 0)
                act.wait_ge(st_q, g * (16 * PARTS))
                for a in range(HALVES):
                    act.wait_ge(pe_q, g * 8 + (4 * a + 4))
                    act.copy(q_out[0][:, :, a, :], ps_o[a][:].rearrange("p (j q) -> p j q", j=GT)
                             ).then_inc(q_hi, 1)
                if more:
                    x_copy(g + 1, 1 - odd, 1)
                for a in range(HALVES):
                    act.wait_ge(q_rested, g * 2 + (a + 1))
                    act.copy(q_out[1][:, :, a, :], q_rest[a][:].rearrange("p (j q) -> p j q", j=GT)
                             ).then_inc(q_mid, 1)

                def value(j):
                    act.wait_ge(pe_v, g * GT + (j + 1))
                    act.wait_ge(kv_rested, g * GT + max(j - 1, 0))
                    act.copy(kv_f[j % 2][:, D:2 * D], ps_t[j % 2][:, 0:D]).then_inc(v_copied, 1)

                def high(j):
                    act.wait_ge(v_copied, g * GT + (j + 1))
                    act.wait_ge(k_done, g * GT + (j + 1))
                    act.wait_ge(st_kv[j], g * 16)
                    act.copy(second_high(kv_out[j]), kv_f[j % 2][:, 0:D].rearrange("p (h d) -> p h d", h=H))
                    act.copy(part_of(kv_out[j], HIGH), heads(kv_f[j % 2])).then_inc(kv_hi, 1)

                def middle(j):
                    act.wait_ge(kv_rested, g * GT + (j + 1))
                    act.copy(part_of(kv_out[j], MID), heads(kv_rest[j % 2])).then_inc(kv_mid, 1)

                value(0)
                for j in range(GT + 1):
                    if j + 1 < GT:
                        value(j + 1)
                    if j < GT:
                        high(j)
                    if j > 0:
                        middle(j - 1)

            for c in range(HALVES):
                x_copy(0, 0, c)
            for g in range(2):
                group(g, g, True)
            with act.Fori(1, G // 2 - 1) as gg:
                for odd in range(2):
                    group(gg * 2 + odd, odd, True)
            group(G - 2, 0, True)
            group(G - 1, 1, False)

            def fe_cast(f8, f16):
                act.wait_ge(ld_adj, f16 + 16)
                act.wait_ge(pe_cnt, f8)
                act.activation(joined[:], adj_in[:], ACT.Sign, bias=minus_half[:]).then_inc(act_cast, 8)

            def joined_group(f8, g):
                act.wait_ge(pe_jt, f8 + 2 * g + 2)
                act.activation(joined_t[:, 8 * g:8 * g + 8, :].rearrange("p b q -> p (b q)"), as_bf16(ps_fe),
                               ACT.Copy, bias=-0.5, scale=0.5).then_inc(act_jt, 2)

            def row_std(l8):
                act.wait_ge(dve_ln, l8 + 3)
                act.activation(std[:], mean_var[:, 1:2], ACT.Sqrt, bias=eps[:]).then_inc(act_std, 8)

            def k_pair(next8, nb, p):
                act.wait_ge(pe_kt, next8 + (2 * p + 2))
                act.copy(k_t[nb][:, 2 * p:2 * p + 2, :].rearrange("p h k -> p (h k)"), as_bf16(ps_k)
                         ).then_inc(act_kt, 2)

            def mask_of(next8, nb):
                act.wait_ge(pe_mask, next8 + 8)
                act.activation(mask[nb][:], ps_k[:], ACT.Identity, bias=be_sb[:]).then_inc(act_mask, 8)

            act.wait_ge(ld_c, 32)
            for f in range(2):
                if f > 0:
                    act.wait_ge(st_mask, 16 * f)
                for g in range(4):
                    joined_group(8 * f, g)
                fe_cast(8 * f + 8, 16 * f + 16)
            mask_of(0, 0)
            for p in range(PAIRS):
                k_pair(0, 0, p)

            def item(b, first, r, it):
                n8, t = act.snap(r["n8"]), act.snap(r["t"])
                next8 = n8 + 8
                nb = (b + 1) % RING
                f8 = t * 8 + 16

                def next_cast():
                    with act.If(act.snap(r["t"]) < T - 3):
                        fe_cast(t * 8 + 24, t * 16 + 48)

                def pair(p):
                    act.wait_ge(pe_hard_t, n8 + (2 * p + 2 + A_HT))
                    act.wait_ge(pe_pv, n8 + (2 * p - 2 + A_PV))
                    act.copy(hard_t[p % 2][:], as_bf16(ps_t[p % 2])).then_inc(act_hard_t, 2)

                def next_k(p):
                    if first:
                        with act.If(act.snap(r["nm"]) > 1):
                            k_pair(next8, nb, p)
                    else:
                        k_pair(next8, nb, p)

                if first:
                    with act.If(act.snap(r["nm"]) > 1):
                        mask_of(next8, nb)
                    def group(g):
                        with act.If(t < T - 2):
                            if g == 0:
                                act.wait_ge(st_mask, t * 16 + 32)
                            joined_group(f8, g)

                    pair(0)
                    next_k(0)
                    group(0)
                    pair(1)
                    next_k(1)
                    group(1)
                    row_std(t * 8)
                    pair(2)
                    next_k(2)
                    group(2)
                    next_k(3)
                    group(3)
                    pair(3)
                    with act.If(act.snap(r["nm"]) < 2):
                        mask_of(next8, nb)
                        for p in range(PAIRS):
                            k_pair(next8, nb, p)
                        next_cast()
                        end_of_tile(act, r)
                else:
                    mask_of(next8, nb)
                    for p in range(PAIRS - 1):
                        pair(p)
                        next_k(p)
                    next_k(3)
                    pair(3)
                    with in_last_item(act, r):
                        next_cast()
                        end_of_tile(act, r)

            run_items(act, item, load_count(act), closing=lambda b, n8: row_std(8 * T))

        @block.vector
        def _(dve):
            dve.memset(zeros[:], 0.0)
            dve.memset(minus_half[:], -0.5)
            dve.memset(eps[:], EPS)
            dve.memset(mean_var[:], 0.0)
            dve.memset(hard_t[1][:], 0.0)
            dve.memset(kv[RING - 1][:, :, 6 * HR:], 0.0)
            dve.memset(q_next[:], 0.0)
            dve.memset(o_run[:], 0.0)
            dve.memset(keep[:], 0.0)
            dve.memset(ones_b[:], 1.0)
            dve.memset(masked[:], -1.0).then_inc(dve_c, 1)
            dve.memset(ones_f[:], 1.0)
            dve.memset(before[:], 1.0).then_inc(dve_c, 1)
            dve.memset(ident_f[:], 1.0).then_inc(dve_c, 1)
            dve.wait_ge(pool_c, 6)
            dve.tensor_copy(iota_h[:], iota[:])
            dve.tensor_scalar(iota_1[:], iota[:, 0:NB], 1.0, None, ALU.add)
            dve.tensor_copy(first_key_f[:], first_key[:])
            dve.tensor_copy(ident_b[:], ident_f[:]).then_inc(dve_c, 1)
            dve.tensor_scalar(ident_big[:], ident_f[:], BIG, None, ALU.mult).then_inc(dve_c, 1)
            for i in range(3):
                dve.wait_ge(pe_w, i + 1)
                if i == 0:
                    for c in range(HALVES):
                        done = dve.tensor_copy(
                            w_t[0][:, c, :].rearrange("p (a d i) -> p a d i", a=HALVES, d=HD),
                            ps_s[0][:, c * D:c * D + D].rearrange("p (i a d) -> p a d i", a=HALVES, d=HD))
                    done.then_inc(dve_w, 1)
                else:
                    dve.tensor_copy(w_t[i][:].rearrange("p a e -> p (a e)"), (ps_s + ps_t)[i][:]).then_inc(dve_w, 1)
            dve.wait_ge(ld_c, 32)
            def group(g):
                for a in range(HALVES):
                    dve.wait_ge(q_hi, g * 2 + (a + 1))
                    dve.tensor_tensor(q_rest[a][:].rearrange("p (j q) -> p j q", j=GT),
                                      ps_o[a][:].rearrange("p (j q) -> p j q", j=GT), q_out[0][:, :, a, :],
                                      ALU.subtract).then_inc(q_rested, 1)
                for a in range(HALVES):
                    dve.wait_ge(q_mid, g * 2 + (a + 1))
                    dve.tensor_tensor(q_out[2][:, :, a, :], q_rest[a][:].rearrange("p (j q) -> p j q", j=GT),
                                      q_out[1][:, :, a, :], ALU.subtract).then_inc(q_low, 1)

                def k_row(j):
                    dve.wait_ge(pe_k, g * GT + (j + 1))
                    dve.wait_ge(kv_rested, g * GT + max(j - 1, 0))
                    dve.scalar_tensor_tensor(out=kv_f[j % 2][:, 0:D], in0=ps_s[j % 2][:, 0:D], scalar=SCALE,
                                             in1=we_sb[:], op0=ALU.mult, op1=ALU.add).then_inc(k_done, 1)

                def rest(j):
                    dve.wait_ge(kv_hi, g * GT + (j + 1))
                    dve.wait_ge(kv_low, g * GT + max(j - 1, 0))
                    dve.tensor_tensor(heads(kv_rest[j % 2]), heads(kv_f[j % 2]), part_of(kv_out[j], HIGH),
                                      ALU.subtract).then_inc(kv_rested, 1)

                def low(j):
                    dve.wait_ge(kv_mid, g * GT + (j + 1))
                    dve.tensor_tensor(part_of(kv_out[j], LOW), heads(kv_rest[j % 2]),
                                      part_of(kv_out[j], MID), ALU.subtract).then_inc(kv_low, 1)

                k_row(0)
                for j in range(GT + 1):
                    if j + 1 < GT:
                        k_row(j + 1)
                    if j < GT:
                        rest(j)
                    if j > 0:
                        low(j - 1)

            group(0)
            with dve.Fori(1, G) as g:
                group(g)

            def fe_scan(f8, f16):
                dve.wait_ge(pe_cnt, f8 + 8)
                dve.tensor_scalar(flag[:], ps_fe[:, 0:NB], 1.0 - P, None, ALU.is_gt).then_inc(dve_fe, 1)
                dve.wait_ge(dve_fe, f16 + 1)
                dve.tensor_reduce(listed[:], flag[:], AX.X, ALU.add).then_inc(dve_fe, 1)
                dve.tensor_tensor(found[0][:], flag[:], iota_1[:], ALU.mult).then_inc(dve_fe, 1)

            def fe_hot(f8, f16, f):
                def top8(i):
                    dve.max(out=order[:, 8 * i:8 * i + 8], in_=found[i % 2][:]).then_inc(dve_fe, 1)

                def without(i):
                    dve.match_replace(out=found[1 - i % 2][:], in_to_replace=order[:, 8 * i:8 * i + 8],
                                      in_values=found[i % 2][:], imm_value=0.0).then_inc(dve_fe, 1)

                dve.wait_ge(pe_base, f8 + 8)
                dve.wait_ge(dve_fe, f16 + 3)
                dve.tensor_scalar(rank0[:], ps_fe[:, 64:65], 0.0, None, ALU.add)
                dve.tensor_scalar(total_i[:], ps_fe[:, 65:66], float(SLOTS - 1), None, ALU.add)
                top8(0)
                dve.wait_ge(dve_fe, f16 + 4)
                dve.tensor_scalar(digits[:, 0:1], rank0[:], P - 1, None, ALU.bitwise_and)
                dve.tensor_scalar(digits[:, 1:2], rank0[:], 7, None, ALU.arith_shift_right)
                without(0)
                dve.wait_ge(dve_fe, f16 + 5)
                dve.tensor_scalar(digits_f[:, 0:1], digits[:, 0:1], float(NB - 1), None, ALU.add)
                dve.tensor_scalar(digits_f[:, 1:2], digits[:, 1:2], 1.0, None, ALU.add)
                top8(1)
                dve.wait_ge(dve_fe, f16 + 6)
                dve.tensor_scalar(hot_lo[:], iota_h[:], digits_f[:, 0:1], None, ALU.is_equal)
                without(1)
                dve.wait_ge(dve_fe, f16 + 7)
                dve.tensor_scalar(hot_hi[:], iota_h[:, 0:NB + 2], digits_f[:, 1:2], None, ALU.is_equal)
                top8(2)
                dve.wait_ge(dve_fe, f16 + 8)
                dve.tensor_scalar(n_items[:, bass.ds(f, 1)], total_i[:], 9, None, ALU.arith_shift_right)
                without(2)
                dve.wait_ge(dve_fe, f16 + 9)
                dve.tensor_scalar(unused[:], slot_id[:], ps_fe[:, 65:66], float(N), ALU.is_ge, ALU.mult)
                top8(3)
                dve.wait_ge(dve_fe, f16 + 10)
                dve.tensor_scalar(real[:], order[:], 0.0, None, ALU.is_gt).then_inc(dve_fe, 1)
                dve.wait_ge(dve_fe, f16 + 11)
                dve.scalar_tensor_tensor(out=keys[:], in0=order[:], scalar=first_key_f[:], in1=real[:],
                                         op0=ALU.add, op1=ALU.mult).then_inc(dve_fe, 1)
                dve.wait_ge(dve_fe, f16 + 12)
                dve.tensor_tensor(hot_key[:], keys[:].unsqueeze(2).to_broadcast([P, NB, NB + 2]),
                                  hot_hi[:].unsqueeze(1).to_broadcast([P, NB, NB + 2]), ALU.mult).then_inc(dve_fe, 1)

            def fe_list(f8, f16, f):
                dve.wait_ge(dve_fe, f16 + 13)
                dve.wait_ge(pe_list, f8 + 8)
                dve.scalar_tensor_tensor(out=list_f[:], in0=ps_fe[:, 128:128 + NB], scalar=float(N // 2),
                                         in1=unused[:], op0=ALU.add, op1=ALU.max).then_inc(dve_fe, 1)
                dve.wait_ge(dve_fe, f16 + 14)
                dve.wait_ge(lists_read, f)
                off = (f % TABLES if isinstance(f, int) else f & (TABLES - 1)) * NB
                dve.tensor_copy(lists[:, bass.ds(off, NB)], list_f[:]).then_inc(dve_fe, 2)

            fe_scan(0, 0)
            fe_hot(0, 0, 0)
            fe_list(0, 0, 0)
            fe_scan(8, 16)
            fe_hot(8, 16, 1)

            def merge(n8):
                for k in range(2):
                    dve.wait_ge(pe_pv, n8 + (4 * k + 4 - 8 + A_PV))
                    dve.tensor_reduce(o_item[:, 4 * k:4 * k + 4, :],
                                      ps_o[k][:, 0:4 * PARTS * HD].rearrange("p (h s d) -> p h d s", h=4, s=PARTS),
                                      AX.X, ALU.add).then_inc(dve_osum, 4)
                dve.wait_ge(dve_merge, n8 + A_MERGE)
                dve.wait_ge(dve_keep, n8 + A_KEEP)
                dve.tensor_tensor(o_run[:], o_run[:], keep[:].unsqueeze(2).to_broadcast([P, H, HD]),
                                  ALU.mult).then_inc(dve_merge, 4)
                dve.wait_ge(dve_osum, n8 + 8)
                dve.wait_ge(dve_merge, n8 + (4 + A_MERGE))
                dve.tensor_tensor(o_run[:], o_run[:], o_item[:], ALU.add).then_inc(dve_merge, 4)

            def norm_stats(l8, l16, n8):
                dve.wait_ge(ld_x0, l16)
                dve.wait_ge(dve_merge, n8 + (8 + A_MERGE))
                dve.scalar_tensor_tensor(out=y[:], in0=o_run[:].rearrange("p h d -> p (h d)"), scalar=1.0 / H,
                                         in1=x_row[:], op0=ALU.mult, op1=ALU.add).then_inc(dve_ln, 1)
                dve.wait_ge(dve_ln, l8 + 1)
                dve.bn_stats(stats[:], y[:]).then_inc(dve_ln, 1)
                wait_alone(dve, (dve_ln, l8 + 2)) if not isinstance(l8, int) else dve.wait_ge(dve_ln, l8 + 2)
                dve.bn_aggr(mean_var[:], stats[:]).then_inc(dve_ln, 1)

            def norm_apply(l8, l16):
                dve.wait_ge(act_std, l8 + 8)
                dve.reciprocal(rstd[:], std[:]).then_inc(dve_ln, 1)
                dve.wait_ge(dve_ln, l8 + 4)
                dve.wait_ge(st_out, l16)
                dve.tensor_scalar(y_out[:], y[:], mean_var[:, 0:1], rstd[:, 0:1], ALU.subtract,
                                  ALU.mult).then_inc(dve_ln, 4)

            def take_q(landed_tiles, scores_done):
                dve.wait_ge(ld_q, landed_tiles)
                dve.wait_ge(pe_score, scores_done)
                dve.tensor_copy(q_cur[:].rearrange("p s h q -> p (s h q)"),
                                q_next[:].rearrange("p s h q -> p (s h q)")).then_inc(q_ready, 1)

            take_q(QLOAD, 0)
            dve.sem_inc(dve_top, A_TOP)
            dve.sem_inc(dve_merge, A_MERGE)
            dve.sem_inc(dve_keep, A_KEEP)
            dve.sem_inc(dve_ln, 8)
            dve.sem_inc(st_out, 16)

            def item(b, first, r, it):
                n8, t = dve.snap(r["n8"]), dve.snap(r["t"])
                nb = (b + 1) % RING
                f8, f16 = t * 8 + 16, t * 16 + 32

                def tops(p):
                    for h in (2 * p, 2 * p + 1):
                        wait_alone(dve, (pe_score, n8 + (h + 1)), *[(act_mask, n8 + 8)][:h == 0])
                        dve.tensor_tensor_reduce(out=score[h % 4][:], in0=ps_s[h % 2][:], in1=mask[b][:], scale=1.0,
                                                 scalar=FLOOR if first else top[b - 1][:, h:h + 1], op0=ALU.add, op1=ALU.max,
                                                 accum_out=top[b][:, h:h + 1]).then_inc(dve_top, 1)

                def hards(p):
                    dve.wait_ge(pe_hard_t, n8 + (2 * p - 2 + A_HT))
                    for h in (2 * p, 2 * p + 1):
                        dve.wait_ge(dve_top, n8 + (h + 1 + A_TOP))
                        if h == H - 1:
                            if first:
                                dve.memset(keep[:], 0.0).then_inc(dve_keep, 8)
                            else:
                                dve.tensor_tensor(keep[:], top[b - 1][:], top[b][:], ALU.is_equal
                                                  ).then_inc(dve_keep, 8)
                        dve.tensor_scalar(hard[h % 4][:], score[h % 4][:], top[b][:, h:h + 1], None,
                                          ALU.is_equal).then_inc(dve_hard, 1)

                for p in range(PAIRS):
                    tops(p)
                    hards(p)
                    if p == 0 and first:
                        with dve.If(t < T - 1):
                            fe_list(t * 8 + 8, t * 16 + 16, t + 1)
                    if p == 1:
                        merge(n8)
                        if first:
                            with dve.If(t > 0):
                                norm_stats(t * 8, t * 16, n8)
                if first:
                    with dve.If(t > 0):
                        norm_apply(t * 8, t * 16)

                def last_item():
                    with dve.If(t < T - 2):
                        fe_scan(f8, f16)
                    with dve.If(t < T - 1):
                        take_q(t * QLOAD + 2 * QLOAD, n8 + 8)
                    with dve.If(t < T - 2):
                        fe_hot(f8, f16, t + 2)
                    end_of_tile(dve, r)

                if first:
                    with dve.If(dve.snap(r["nm"]) < 2):
                        last_item()
                else:
                    with in_last_item(dve, r):
                        last_item()

            def closing(b, n8):
                merge(n8)
                norm_stats(8 * T, 16 * T, n8)
                norm_apply(8 * T, 16 * T)
            run_items(dve, item, load_count(dve), closing=closing)

        @block.tensor
        def _(pe):
            pe.wait_ge(pool_c, 6)
            pe.wait_ge(dve_c, 5)
            for k in range(2):
                mm = pe.matmul(ps_o[k][:, 0:384], ident_b[:], zeros[:, 0:384], start=True, stop=True)
            mm.then_inc(pe_pv, A_PV - 2)
            pe.wait_ge(ld_w, 48)
            for i in range(3):
                for a in range(HALVES):
                    for c in range(HALVES):
                        mm = pe.transpose((ps_s + ps_t)[i][:, c * D + a * P:c * D + a * P + P],
                                          w_sb[i][:, a, c * P:c * P + P], ident_f[:])
                mm.then_inc(pe_w, 1)
            pe.wait_ge(dve_w, 3)
            pe.wait_ge(pe_pv, A_PV - 2)
            def x_half(g, uses, odd, c):
                if c == 0:
                    pe.wait_ge(ld_x[odd], uses)
                pe.wait_ge(xt_copied, g * 2 + c)
                for j in range(GT):
                    mm = pe.transpose(ps_k[:, j * P:j * P + P], x_in[odd][:, j, c * P:c * P + P], ident_f[:])
                mm.then_inc(pe_xt, 1)

            def group(g, gg, odd, more):
                if more:
                    x_half(g + 1, (gg + odd) * 16 + 16, 1 - odd, 0)
                pe.wait_ge(xt_copied, g * 2 + 2)
                pe.wait_ge(q_rested, g * 2)
                for a in range(HALVES):
                    for c in range(HALVES):
                        mm = pe.matmul(ps_o[a][:], w_t[0][:, c, a * P:a * P + P], x_t[odd][:, c, :],
                                       start=(c == 0), stop=(c == 1))
                    mm.then_inc(pe_q, 4)
                if more:
                    x_half(g + 1, (gg + odd) * 16 + 16, 1 - odd, 1)
                for j in range(GT):
                    pe.wait_ge(k_done, g * GT + max(j - 1, 0))
                    pe.wait_ge(v_copied, g * GT + max(j - 1, 0))
                    for i, bank, done in ((1, ps_s, pe_k), (2, ps_t, pe_v)):
                        for c in range(HALVES):
                            mm = pe.matmul(bank[j % 2][:, 0:D], x_t[odd][:, c, j * P:j * P + P], w_t[i][:, c, :],
                                           start=(c == 0), stop=(c == 1))
                        mm.then_inc(done, 1)

            for c in range(HALVES):
                x_half(0, 16, 0, c)
            for g in range(2):
                group(g, 0, g, True)
            with pe.Fori(1, G // 2 - 1) as gg:
                for odd in range(2):
                    group(gg * 2 + odd, gg, odd, True)
            group(G - 2, G // 2 - 1, 0, True)
            group(G - 1, G // 2 - 1, 1, False)

            blocks = joined[:].rearrange("q (p b) -> q b p", b=NB)

            def fe_transpose(f8, f16, g):
                if g == 0:
                    pe.wait_ge(act_cast, f8 + 8)
                    pe.wait_ge(dve_fe, f16)
                else:
                    pe.wait_ge(act_jt, f8 + 2 * g)
                for b in range(8):
                    mm = pe.transpose(as_bf16(ps_fe)[:, b * P:b * P + P], blocks[:, 8 * g + b, :], ident_b[:])
                mm.then_inc(pe_jt, 2)

            def fe_count(f8):
                pe.wait_ge(act_jt, f8 + 8)
                for b in range(NB):
                    mm = pe.matmul(ps_fe[:, b:b + 1], blocks[:, b, :], ones_b[:], start=True, stop=True)
                mm.then_inc(pe_cnt, 8)

            def fe_base(f8, f16):
                pe.wait_ge(dve_fe, f16 + 2)
                pe.matmul(ps_fe[:, 64:65], before[:], listed[:], start=True, stop=True)
                pe.matmul(ps_fe[:, 65:66], ones_f[:], listed[:], start=True,
                          stop=True).then_inc(pe_base, 8)

            def fe_list(f8, f16):
                pe.wait_ge(dve_fe, f16 + 13)
                for j in range(NB):
                    at = NB - 1 - j
                    pe.matmul(ps_fe[:, 128:129 + NB], hot_lo[:, at:at + P], hot_key[:, j, 1:NB + 2], start=(j == 0),
                              stop=False)
                    mm = pe.matmul(ps_fe[:, 128:129 + NB], hot_lo[:, at + P:at + 2 * P], hot_key[:, j, 0:NB + 1],
                                   start=False, stop=(j == NB - 1))
                mm.then_inc(pe_list, 8)

            def k_pair(n8, nb, p):
                if p == 0:
                    pe.wait_ge(act_mask, n8 + 8)
                else:
                    pe.wait_ge(act_kt, n8 + 2 * p)
                for h in (2 * p, 2 * p + 1):
                    for c in range(CHUNKS):
                        at = (h % 2) * SLOTS + c * P
                        mm = pe.transpose(as_bf16(ps_k)[:, at:at + P], kv[nb][:, c, h * HR:h * HR + P], ident_b[:])
                mm.then_inc(pe_kt, 2)

            def mask_rows(n8, nb, uses):
                pe.wait_ge(landed[nb], uses)
                pe.wait_ge(act_kt, n8)
                for c in range(CHUNKS):
                    mm = pe.matmul(ps_k[:, c * P:c * P + P], mrow[nb][:, c, :], ident_big[:], start=True, stop=True)
                mm.then_inc(pe_mask, 8)

            def scores(n8, b, h):
                pe.wait_ge(dve_top, n8 + (h - 1 + A_TOP))
                if h % 2 == 0:
                    pe.wait_ge(act_kt, n8 + (h + 2))
                for i in range(STACKS):
                    mm = pe.matmul(ps_s[h % 2][:], q_cur[:, i, h, :], k_t[b][:, h, :], start=(i == 0),
                                   stop=(i == STACKS - 1))
                mm.then_inc(pe_score, 1)

            def values(n8, b, p):
                at8 = n8 + 8
                pe.wait_ge(act_hard_t, at8 + (2 * p + 2 + A_HC - 8))
                if p % 2 == 0:
                    pe.wait_ge(dve_osum, at8 + (2 * p + 4 - 8))
                for h in (2 * p, 2 * p + 1):
                    for c in range(CHUNKS):
                        at = (h % 2) * SLOTS + c * P
                        mm = pe.matmul(ps_o[h // 4][:, (h % 4) * HP:(h % 4 + 1) * HP],
                                       hard_t[p % 2][:, at:at + P],
                                       kv[b][:, c, h * HR + P:(h + 1) * HR],
                                       start=(c == 0), stop=(c == CHUNKS - 1))
                mm.then_inc(pe_pv, 2)

            for f in range(2):
                for g in range(4):
                    fe_transpose(8 * f, 16 * f, g)
                fe_count(8 * f)
                fe_base(8 * f, 16 * f)
                if f == 0:
                    fe_list(0, 0)
            mask_rows(0, 0, 128)
            for p in range(PAIRS):
                k_pair(0, 0, p)
            pe.sem_inc(pe_hard_t, A_HT)
            pe.sem_inc(act_hard_t, A_HC)
            pe.wait_ge(q_ready, 1)
            scores(0, 0, 0)
            scores(0, 0, 1)

            def item(b, first, r, it):
                n8, t = pe.snap(r["n8"]), pe.snap(r["t"])
                next8 = n8 + 8
                nb = (b + 1) % RING
                uses = it * 128 + (128 if b < RING - 1 else 256)
                f8, f16 = t * 8 + 16, t * 16 + 32

                def transposes(p):
                    pe.wait_ge(dve_hard, n8 + (2 * p + 2))
                    pe.wait_ge(act_hard_t, n8 + (2 * p - 2 + A_HC))
                    for h in (2 * p, 2 * p + 1):
                        for c in range(CHUNKS):
                            at = (h % 2) * SLOTS + c * P
                            mm = pe.transpose(as_bf16(ps_t[p % 2])[:, at:at + P], hard[h % 4][:, c * P:c * P + P],
                                              ident_b[:])
                    mm.then_inc(pe_hard_t, 2)

                def next_tile_q():
                    with pe.If(pe.snap(r["t"]) < T):
                        pe.wait_ge(q_ready, pe.snap(r["t"]) + 1)

                def next_k(p):
                    if first:
                        with pe.If(pe.snap(r["nm"]) > 1):
                            k_pair(next8, nb, p)
                    else:
                        k_pair(next8, nb, p)

                def front_end(before, stage):
                    if first:
                        with pe.If(t < before):
                            stage()

                front_end(T - 1, lambda: fe_list(t * 8 + 8, t * 16 + 16))
                scores(n8, b, 2)
                scores(n8, b, 3)
                values(n8 - 8, (b - 1) % RING, 3)
                if first:
                    with pe.If(pe.snap(r["nm"]) > 1):
                        mask_rows(next8, nb, uses)
                else:
                    mask_rows(next8, nb, uses)
                transposes(0)
                next_k(0)
                front_end(T - 2, lambda: fe_transpose(f8, f16, 0))
                scores(n8, b, 4)
                scores(n8, b, 5)
                transposes(1)
                next_k(1)
                front_end(T - 2, lambda: fe_transpose(f8, f16, 1))
                values(n8, b, 0)
                scores(n8, b, 6)
                scores(n8, b, 7)
                transposes(2)
                next_k(2)
                if first:
                    with pe.If(pe.snap(r["nm"]) > 1):
                        scores(next8, nb, 0)
                        scores(next8, nb, 1)
                    front_end(T - 2, lambda: fe_transpose(f8, f16, 2))
                else:
                    with in_last_item(pe, r):
                        with pe.If(t < T - 2):
                            fe_count(f8)
                            fe_base(f8, f16)
                        end_of_tile(pe, r)
                        next_tile_q()
                    scores(next8, nb, 0)
                    scores(next8, nb, 1)
                values(n8, b, 1)
                next_k(3)
                front_end(T - 2, lambda: fe_transpose(f8, f16, 3))
                transposes(3)
                values(n8, b, 2)
                if first:
                    with pe.If(pe.snap(r["nm"]) < 2):
                        with pe.If(t < T - 2):
                            fe_count(f8)
                            fe_base(f8, f16)
                        mask_rows(next8, nb, uses)
                        for p in range(PAIRS):
                            k_pair(next8, nb, p)
                        end_of_tile(pe, r)
                        next_tile_q()
                        scores(next8, nb, 0)
                        scores(next8, nb, 1)

            run_items(pe, item, load_count(pe), closing=lambda b, n8: values(n8 - 8, (b - 1) % RING, 3))


_INS = ["x", "adj", "L0_gnn_WQ", "L0_gnn_WK", "L0_gnn_WV", "L0_gnn_we", "L0_gnn_be"]


def kernel(**inputs):
    import numpy as np
    import concourse.bacc as bacc
    from concourse.bass_utils import run_bass_kernel_spmd

    nc = bacc.Bacc("TRN2", target_bir_lowering=False, num_devices=1)
    arrays, args = {}, []
    for name in _INS:
        a = np.ascontiguousarray(inputs[name])
        arrays[f"in_{name}"] = a
        args.append(nc.dram_tensor(f"in_{name}", a.shape, mybir.dt.from_np(a.dtype), kind="ExternalInput").ap())
    args.append(nc.dram_tensor("out_0", inputs["x"].shape, mybir.dt.float32, kind="ExternalOutput").ap())
    hard_attention(nc, *args)
    r = run_bass_kernel_spmd(nc, [arrays], core_ids=[0])
    return r.results[0]["out_0"]
```
